# Optimizing a Trainium2 kernel written in Bass

```python
import numpy as np
import jax
import jax.numpy as jnp

def _softmax(x, axis=-1):
    return jax.nn.softmax(x, axis=axis)

def _gelu(x):
    return jax.nn.gelu(x, approximate=True)

def _silu(x):
    return jax.nn.silu(x)

def _sigmoid(x):
    return jax.nn.sigmoid(x)

def _layernorm(x, axis=-1, eps=1e-05):
    m = jnp.mean(x, axis=axis, keepdims=True)
    v = jnp.var(x, axis=axis, keepdims=True)
    return (x - m) / jnp.sqrt(v + eps)

def _scatter_add(tgt, idx, src, axis=0):
    return tgt.at[idx].add(src)

def _segment_sum(src, seg, n):
    return jax.ops.segment_sum(src, seg, n)
kernel_name = 'mk_dlrm_tower_d1_rec_r8_b6ca8d'

def setup_inputs(seed: int=0):
    np.random.seed(seed)
    _w = jnp.asarray

    def _rec_inputs():
        import jax
        import jax.numpy as jnp
        _tk = jax.random.key(seed)
        ids = jnp.stack([jax.random.randint(jax.random.fold_in(_tk, 200 + f), (512,), 0, v, jnp.int32) for f, v in enumerate([12500, 1250, 125000, 1250, 1000, 12500, 1000, 1000, 12500, 12500, 125000, 125000, 12500, 12500, 12500, 1250, 1250, 1000, 12500, 1000, 1250, 1000, 1250, 1000, 1250, 1250])], axis=1)
        tbl_0 = 0.05 * jax.random.normal(jax.random.fold_in(_tk, 500 + 0), (12500, 64), jnp.float32)
        tbl_1 = 0.05 * jax.random.normal(jax.random.fold_in(_tk, 500 + 1), (1250, 64), jnp.float32)
        tbl_2 = 0.05 * jax.random.normal(jax.random.fold_in(_tk, 500 + 2), (125000, 64), jnp.float32)
        tbl_3 = 0.05 * jax.random.normal(jax.random.fold_in(_tk, 500 + 3), (1250, 64), jnp.float32)
        tbl_4 = 0.05 * jax.random.normal(jax.random.fold_in(_tk, 500 + 4), (1000, 64), jnp.float32)
        tbl_5 = 0.05 * jax.random.normal(jax.random.fold_in(_tk, 500 + 5), (12500, 64), jnp.float32)
        tbl_6 = 0.05 * jax.random.normal(jax.random.fold_in(_tk, 500 + 6), (1000, 64), jnp.float32)
        tbl_7 = 0.05 * jax.random.normal(jax.random.fold_in(_tk, 500 + 7), (1000, 64), jnp.float32)
        tbl_8 = 0.05 * jax.random.normal(jax.random.fold_in(_tk, 500 + 8), (12500, 64), jnp.float32)
        tbl_9 = 0.05 * jax.random.normal(jax.random.fold_in(_tk, 500 + 9), (12500, 64), jnp.float32)
        tbl_10 = 0.05 * jax.random.normal(jax.random.fold_in(_tk, 500 + 10), (125000, 64), jnp.float32)
        tbl_11 = 0.05 * jax.random.normal(jax.random.fold_in(_tk, 500 + 11), (125000, 64), jnp.float32)
        tbl_12 = 0.05 * jax.random.normal(jax.random.fold_in(_tk, 500 + 12), (12500, 64), jnp.float32)
        tbl_13 = 0.05 * jax.random.normal(jax.random.fold_in(_tk, 500 + 13), (12500, 64), jnp.float32)
        tbl_14 = 0.05 * jax.random.normal(jax.random.fold_in(_tk, 500 + 14), (12500, 64), jnp.float32)
        tbl_15 = 0.05 * jax.random.normal(jax.random.fold_in(_tk, 500 + 15), (1250, 64), jnp.float32)
        tbl_16 = 0.05 * jax.random.normal(jax.random.fold_in(_tk, 500 + 16), (1250, 64), jnp.float32)
        tbl_17 = 0.05 * jax.random.normal(jax.random.fold_in(_tk, 500 + 17), (1000, 64), jnp.float32)
        tbl_18 = 0.05 * jax.random.normal(jax.random.fold_in(_tk, 500 + 18), (12500, 64), jnp.float32)
        tbl_19 = 0.05 * jax.random.normal(jax.random.fold_in(_tk, 500 + 19), (1000, 64), jnp.float32)
        tbl_20 = 0.05 * jax.random.normal(jax.random.fold_in(_tk, 500 + 20), (1250, 64), jnp.float32)
        tbl_21 = 0.05 * jax.random.normal(jax.random.fold_in(_tk, 500 + 21), (1000, 64), jnp.float32)
        tbl_22 = 0.05 * jax.random.normal(jax.random.fold_in(_tk, 500 + 22), (1250, 64), jnp.float32)
        tbl_23 = 0.05 * jax.random.normal(jax.random.fold_in(_tk, 500 + 23), (1000, 64), jnp.float32)
        tbl_24 = 0.05 * jax.random.normal(jax.random.fold_in(_tk, 500 + 24), (1250, 64), jnp.float32)
        tbl_25 = 0.05 * jax.random.normal(jax.random.fold_in(_tk, 500 + 25), (1250, 64), jnp.float32)
        _rk = jax.random.fold_in(_tk, 7)
        r_dense_t = 7.22013e-05 + 1.00017 * jax.random.normal(jax.random.fold_in(_rk, 101), (512, 256), jnp.float32)
        W_top1 = 0.0360844 * jax.random.normal(jax.random.fold_in(_tk, 801), (768, 512), jnp.float32)
        W_top2 = 0.0441942 * jax.random.normal(jax.random.fold_in(_tk, 802), (512, 256), jnp.float32)
        W_top3 = 0.0625 * jax.random.normal(jax.random.fold_in(_tk, 803), (256, 1), jnp.float32)
        b_top1 = jnp.zeros((512,), jnp.float32)
        b_top2 = jnp.zeros((256,), jnp.float32)
        return (r_dense_t, ids, tbl_0, tbl_1, tbl_2, tbl_3, tbl_4, tbl_5, tbl_6, tbl_7, tbl_8, tbl_9, tbl_10, tbl_11, tbl_12, tbl_13, tbl_14, tbl_15, tbl_16, tbl_17, tbl_18, tbl_19, tbl_20, tbl_21, tbl_22, tbl_23, tbl_24, tbl_25, W_top1, b_top1, W_top2, b_top2, W_top3)
    r_dense_t, ids, tbl_0, tbl_1, tbl_2, tbl_3, tbl_4, tbl_5, tbl_6, tbl_7, tbl_8, tbl_9, tbl_10, tbl_11, tbl_12, tbl_13, tbl_14, tbl_15, tbl_16, tbl_17, tbl_18, tbl_19, tbl_20, tbl_21, tbl_22, tbl_23, tbl_24, tbl_25, W_top1, b_top1, W_top2, b_top2, W_top3 = _rec_inputs()

    def _L0_rec_setup():
        import jax, jax.numpy as jnp
        import numpy as np
        EPS = 1e-05
        NI = 33
        TRIL_I, TRIL_J = np.tril_indices(NI, k=-1)

        def layer_norm(x, g, b):
            m = jnp.mean(x, axis=-1, keepdims=True)
            v = jnp.mean(jnp.square(x - m), axis=-1, keepdims=True)
            return (x - m) * jax.lax.rsqrt(v + EPS) * g + b
        key = jax.random.key(seed)
        ks = jax.random.split(key, 8)
        B, D_DENSE, N_SP, D_SP = (4096, 256, 26, 64)
        E, PROJ, MAXD, NFLAT = (128, 32, 512, 528)
        dense_t = jax.random.normal(ks[0], (B, D_DENSE), dtype=jnp.float32)
        sparse_t = jax.random.normal(ks[1], (B, N_SP, D_SP), dtype=jnp.float32)
        Wd = jax.random.normal(ks[2], (E, D_DENSE), dtype=jnp.float32) / np.sqrt(D_DENSE)
        Ws = jax.random.normal(ks[3], (E, D_SP), dtype=jnp.float32) / np.sqrt(D_SP)
        Wsi = jax.random.normal(ks[4], (PROJ, N_SP), dtype=jnp.float32) / np.sqrt(N_SP)
        Wl = jax.random.normal(ks[5], (MAXD, NFLAT), dtype=jnp.float32) / np.sqrt(NFLAT)
        gd = jnp.ones((E,), jnp.float32)
        bd = jnp.zeros((E,), jnp.float32)
        gs = jnp.ones((E,), jnp.float32)
        bs = jnp.zeros((E,), jnp.float32)
        gsi = jnp.ones((PROJ,), jnp.float32)
        bsi = jnp.zeros((PROJ,), jnp.float32)
        gl = jnp.ones((MAXD,), jnp.float32)
        bl = jnp.zeros((MAXD,), jnp.float32)
        return {'dense_t': dense_t, 'sparse_t': sparse_t, 'Wd': Wd, 'gd': gd, 'bd': bd, 'Ws': Ws, 'gs': gs, 'bs': bs, 'Wsi': Wsi, 'gsi': gsi, 'bsi': bsi, 'Wl': Wl, 'gl': gl, 'bl': bl, 'dims_in_use': 384}
    _L0_rec_all = _L0_rec_setup()
    _L0_rec_in = {k: v for k, v in _L0_rec_all.items() if k in ('Wd', 'gd', 'bd', 'Ws', 'gs', 'bs', 'Wsi', 'gsi', 'bsi', 'Wl', 'gl', 'bl')}
    del _L0_rec_all
    return {'r_dense_t': r_dense_t, 'ids': ids, 'tbl_0': tbl_0, 'tbl_1': tbl_1, 'tbl_2': tbl_2, 'tbl_3': tbl_3, 'tbl_4': tbl_4, 'tbl_5': tbl_5, 'tbl_6': tbl_6, 'tbl_7': tbl_7, 'tbl_8': tbl_8, 'tbl_9': tbl_9, 'tbl_10': tbl_10, 'tbl_11': tbl_11, 'tbl_12': tbl_12, 'tbl_13': tbl_13, 'tbl_14': tbl_14, 'tbl_15': tbl_15, 'tbl_16': tbl_16, 'tbl_17': tbl_17, 'tbl_18': tbl_18, 'tbl_19': tbl_19, 'tbl_20': tbl_20, 'tbl_21': tbl_21, 'tbl_22': tbl_22, 'tbl_23': tbl_23, 'tbl_24': tbl_24, 'tbl_25': tbl_25, 'W_top1': W_top1, 'b_top1': b_top1, 'W_top2': W_top2, 'b_top2': b_top2, 'W_top3': W_top3, 'L0_rec_Wd': _L0_rec_in['Wd'], 'L0_rec_gd': _L0_rec_in['gd'], 'L0_rec_bd': _L0_rec_in['bd'], 'L0_rec_Ws': _L0_rec_in['Ws'], 'L0_rec_gs': _L0_rec_in['gs'], 'L0_rec_bs': _L0_rec_in['bs'], 'L0_rec_Wsi': _L0_rec_in['Wsi'], 'L0_rec_gsi': _L0_rec_in['gsi'], 'L0_rec_bsi': _L0_rec_in['bsi'], 'L0_rec_Wl': _L0_rec_in['Wl'], 'L0_rec_gl': _L0_rec_in['gl'], 'L0_rec_bl': _L0_rec_in['bl']}

def reference(r_dense_t, ids, tbl_0, tbl_1, tbl_2, tbl_3, tbl_4, tbl_5, tbl_6, tbl_7, tbl_8, tbl_9, tbl_10, tbl_11, tbl_12, tbl_13, tbl_14, tbl_15, tbl_16, tbl_17, tbl_18, tbl_19, tbl_20, tbl_21, tbl_22, tbl_23, tbl_24, tbl_25, W_top1, b_top1, W_top2, b_top2, W_top3, L0_rec_Wd, L0_rec_gd, L0_rec_bd, L0_rec_Ws, L0_rec_gs, L0_rec_bs, L0_rec_Wsi, L0_rec_gsi, L0_rec_bsi, L0_rec_Wl, L0_rec_gl, L0_rec_bl):
    import jax
    import jax.numpy as jnp

    def _L0_rec_ref(dense_t, sparse_t, Wd, gd, bd, Ws, gs, bs, Wsi, gsi, bsi, Wl, gl, bl, dims_in_use):
        import jax, jax.numpy as jnp
        import numpy as np
        EPS = 1e-05
        NI = 33
        TRIL_I, TRIL_J = np.tril_indices(NI, k=-1)

        def layer_norm(x, g, b):
            m = jnp.mean(x, axis=-1, keepdims=True)
            v = jnp.mean(jnp.square(x - m), axis=-1, keepdims=True)
            return (x - m) * jax.lax.rsqrt(v + EPS) * g + b
        x = layer_norm(dense_t @ Wd.T, gd, bd)
        y = layer_norm(jnp.einsum('bnd,ed->bne', sparse_t, Ws), gs, bs)
        y = jnp.einsum('bne,pn->bep', y, Wsi)
        y = layer_norm(y, gsi, bsi)
        y = jnp.swapaxes(y, 1, 2)
        T = jnp.concatenate([x[:, None, :], y], axis=1)
        Z = jnp.einsum('bnd,bmd->bnm', T, T)
        Zflat = Z[:, TRIL_I, TRIL_J]
        out = layer_norm(Zflat @ Wl.T, gl, bl)
        maxd = out.shape[-1]
        mask = (jnp.arange(maxd) < dims_in_use).astype(out.dtype)
        return out * mask
    e = jnp.stack([tbl_0[ids[:, 0]], tbl_1[ids[:, 1]], tbl_2[ids[:, 2]], tbl_3[ids[:, 3]], tbl_4[ids[:, 4]], tbl_5[ids[:, 5]], tbl_6[ids[:, 6]], tbl_7[ids[:, 7]], tbl_8[ids[:, 8]], tbl_9[ids[:, 9]], tbl_10[ids[:, 10]], tbl_11[ids[:, 11]], tbl_12[ids[:, 12]], tbl_13[ids[:, 13]], tbl_14[ids[:, 14]], tbl_15[ids[:, 15]], tbl_16[ids[:, 16]], tbl_17[ids[:, 17]], tbl_18[ids[:, 18]], tbl_19[ids[:, 19]], tbl_20[ids[:, 20]], tbl_21[ids[:, 21]], tbl_22[ids[:, 22]], tbl_23[ids[:, 23]], tbl_24[ids[:, 24]], tbl_25[ids[:, 25]]], axis=1)
    z = _L0_rec_ref(r_dense_t, e, L0_rec_Wd, L0_rec_gd, L0_rec_bd, L0_rec_Ws, L0_rec_gs, L0_rec_bs, L0_rec_Wsi, L0_rec_gsi, L0_rec_bsi, L0_rec_Wl, L0_rec_gl, L0_rec_bl, 384)
    z = z.reshape(z.shape[0], -1)
    h = jnp.concatenate([z, r_dense_t], axis=1)
    h = jnp.maximum(h @ W_top1 + b_top1, 0.0)
    h = jnp.maximum(h @ W_top2 + b_top2, 0.0)
    y = h @ W_top3
    return y

_drawn_inputs = setup_inputs


def setup_inputs(seed=0):
    import zlib

    import numpy as np

    out = dict(_drawn_inputs(seed))
    spreads = {'b_top1': (0.0, 0.1),
     'b_top2': (0.0, 0.1),
     'L0_rec_gd': (1.0, 0.6),
     'L0_rec_bd': (0.0, 0.8),
     'L0_rec_gs': (1.0, 0.6),
     'L0_rec_bs': (0.0, 0.1),
     'L0_rec_gsi': (1.0, 0.2),
     'L0_rec_bsi': (0.0, 0.1),
     'L0_rec_gl': (1.0, 0.2),
     'L0_rec_bl': (0.0, 0.1)}
    factors = {}
    for name, (base, spread) in spreads.items():
        noise = np.random.default_rng([zlib.crc32(name.encode()), seed]).standard_normal(out[name].shape)
        drawn = base * np.exp(spread * noise) if base else spread * noise
        out[name] = jnp.asarray(drawn.astype(out[name].dtype))
    for name, factor in factors.items():
        out[name] = (out[name] * factor).astype(out[name].dtype)
    return out
```

```python
from contextlib import ExitStack

import concourse.bass as bass
from concourse import mybir

F32 = mybir.dt.float32
BF16 = mybir.dt.bfloat16
I32 = mybir.dt.int32
ALU = mybir.AluOpType
ACT = mybir.ActivationFunctionType
AX_X = mybir.AxisListType.X

P = 128
BATCH = 512
FIELDS = 26
DIM = 64
EMB = 128
PROJ = 32
DENSE = 256
MAXD = 512
KEPT = 384
HID1, HID2 = 512, 256
EPS = 1e-5

TILES = BATCH // P
HALF = P // 2
PAIRS = HALF * FIELDS // P
CHUNKS = 4
CB = HALF // CHUNKS
BANK = CB * PROJ
TOUCH = 6
ITEM = PROJ + 2
GROUPS = P // 4
CG = CB // 4
JX = PROJ // 4
ROW_SUMX, ROW_ONE = 32, 96
PARTS = 3


def chunk_pairs(c):
    last = [((c1 + 1) * CB * FIELDS - 1) // P for c1 in range(CHUNKS)]
    return range(0 if c == 0 else last[c - 1] + 1, last[c] + 1)


def touched(s):
    return P * s // FIELDS, (P * s + P - 1) // FIELDS


MOST = max(len(chunk_pairs(c)) for c in range(CHUNKS))


def build(nc, a, out):
    with ExitStack() as ctx:
        def sb(name, shape, dt=F32):
            return ctx.enter_context(nc.sbuf_tensor(name, shape, dt))

        def bank(name):
            return ctx.enter_context(nc.psum_tensor(name, [P, 512], F32))

        def sem(name):
            return ctx.enter_context(nc.semaphore(name))

        ids = sb("ids", [P, TILES * 2 * PAIRS], I32)
        base = sb("base", [P, 2 * PAIRS], I32)
        index = sb("index", [P, TILES * 2 * PAIRS], I32)
        ident = sb("ident", [P, P])
        center = sb("center", [P, P])
        ws = sb("ws", [EMB, DIM])
        gs = sb("gs", [EMB, 1])
        wc = sb("wc", [EMB, 2, DIM])
        wg = sb("wg", [EMB, 2, DIM])
        gram_w = sb("gram_w", [P, P])
        wg_half = sb("wg_half", [P, 2, EMB])
        wsi = sb("wsi", [P, PAIRS, PROJ])
        wsi_mean = sb("wsi_mean", [P, PAIRS])
        touch = sb("touch", [P, PAIRS, TOUCH])
        wt = sb("wt", [P, PAIRS, TOUCH, PROJ])
        wsi9 = sb("wsi9", [9, PROJ, FIELDS])
        bs9 = sb("bs9", [9, EMB])
        part9 = sb("part9", [9, 2 * PARTS])
        wsum9 = sb("wsum9", [9, PROJ])
        wmean9 = sb("wmean9", [9, 1])
        split_h = sb("split_h", [9, PARTS, EMB], BF16)
        split_r = sb("split_r", [9, 2, EMB])
        split_t = sb("split_t", [9, 2, EMB])
        bias_w = sb("bias_w", [9, PROJ], BF16)
        bias_l = sb("bias_l", [P, EMB], BF16)
        bias_r = sb("bias_r", [P, CB, PROJ], BF16)
        dense_t = sb("dense_t", [P, 2, BATCH])
        wd = sb("wd", [P, 2, EMB])
        gdb = sb("gdb", [EMB, 2])
        x_stats = sb("x_stats", [P, TILES, 6])
        x_mv = sb("x_mv", [P, TILES, 2])
        x_sd = sb("x_sd", [P, TILES])
        x_rs = sb("x_rs", [P, TILES])
        xn = sb("xn", [P, TILES, EMB])
        x_t = sb("x_t", [EMB, BATCH])
        ones = sb("ones", [P, 1])
        eps = sb("eps", [P, 1])
        sumx = sb("sumx", [P, BATCH])
        wl = sb("wl", [P, JX, MAXD])
        we = sb("we", [P, JX, MAXD])
        wx = sb("wx", [P, MAXD])
        fold = sb("fold", [P, 2 + 2 * JX])
        scale_w = sb("scale_w", [P, JX])
        row_scale = sb("row_scale", [P, 1])
        is_row = sb("is_row", [P, PROJ])
        is_col = sb("is_col", [P, JX, PROJ])
        is_x = sb("is_x", [P, JX])
        mix = sb("mix", [P, JX, P])
        mix_t = sb("mix_t", [P, JX, PROJ])
        glb = sb("glb", [P, 2, KEPT // P])
        w1 = sb("w1", [P, (KEPT + DENSE) // P, HID1])
        b1 = sb("b1", [P, HID1 // P])
        w2 = sb("w2", [P, HID1 // P, HID2])
        b2 = sb("b2", [P, HID2 // P])
        w3 = sb("w3", [P, HID2 // P])

        e = sb("e", [P, 2 * PAIRS, DIM])
        e_t = sb("e_t", [P, 2, MOST * P])
        prod = sb("prod", [P, MOST * P])
        ss = sb("ss", [P, 2 * MOST])
        var = sb("var", [P, 2 * MOST])
        sd = sb("sd", [P, 2 * MOST])
        rs = sb("rs", [P, 2 * MOST])
        u = sb("u", [P, 2, BANK])
        sq = sb("sq", [P, 2, BANK])
        ss2 = sb("ss2", [P, 2, CB])
        sd2 = sb("sd2", [P, 2, CB])
        rs2 = sb("rs2", [P, 2, CB])
        items = sb("items", [EMB, CHUNKS, 2, CB, ITEM])
        z_s = sb("z_s", [P, GROUPS, ITEM])
        z_q = sb("z_q", [P, JX, P])
        z_x = sb("z_x", [P, P])
        o_stats = sb("o_stats", [P, 6])
        o_mv = sb("o_mv", [P, 2])
        o_sd = sb("o_sd", [P, 1])
        o_rs = sb("o_rs", [P, 1])
        z = sb("z", [P, KEPT])
        h0 = sb("h0", [P, KEPT // P, P])
        h1 = sb("h1", [P, HID1 // P, P])
        h2 = sb("h2", [P, HID2 // P, P])
        y_row = sb("y_row", [1, BATCH])

        p_tr, p_eg, p_gr, p_o = bank("p_tr"), bank("p_eg"), bank("p_gr"), bank("p_o")
        p_u = [bank("p_u0"), bank("p_u1")]
        p_y = [bank("p_y0"), bank("p_y1")]

        ids_in, early_in, x_in, bias_in, wl_in, mlp_in = (
            sem(n) for n in ("ids_in", "early_in", "x_in", "bias_in", "wl_in", "mlp_in"))
        index_ready = sem("index_ready")
        gathered = [sem(f"gathered{c}") for c in range(CHUNKS)]
        dve_setup = sem("dve_setup")
        pe_wc, pe_gram, pe_wg = sem("pe_wc"), sem("pe_gram"), sem("pe_wg")
        wc_ready, wg_ready, gram_ready, half_ready = (
            sem(n) for n in ("wc_ready", "wg_ready", "gram_ready", "half_ready"))
        wt_ready, bias_ready, mix_ready, ones_ready, eps_ready = (
            sem(n) for n in ("wt_ready", "bias_ready", "mix_ready", "ones_ready", "eps_ready"))
        items_one, zx_clear = sem("items_one"), sem("zx_clear")
        pe_x, x_agg, x_root, xn_ready, pe_xt, xt_ready, pe_sumx, sumx_ready = (
            sem(n) for n in ("pe_x", "x_agg", "x_root", "xn_ready", "pe_xt", "xt_ready",
                             "pe_sumx", "sumx_ready"))
        pe_wx, scale_ready, we_ready, wx_ready = (
            sem(n) for n in ("pe_wx", "scale_ready", "we_ready", "wx_ready"))
        tr_done, et_copied, eg_done, prod_done, ss_done, var_done, sd_done, rs_done, e_scaled = (
            sem(n) for n in ("tr_done", "et_copied", "eg_done", "prod_done", "ss_done", "var_done",
                             "sd_done", "rs_done", "e_scaled"))
        u_done, u_copied, y_done, sq_done, ss2_done, sd2_done, rs2_done, y_normed = (
            sem(n) for n in ("u_done", "u_copied", "y_done", "sq_done", "ss2_done", "sd2_done",
                             "rs2_done", "y_normed"))
        x_placed, gr_done, gr_copied, moved, sumx_placed = (
            sem(n) for n in ("x_placed", "gr_done", "gr_copied", "moved", "sumx_placed"))
        fin_done, o_stat, o_agg, o_root, o_recip, z_ready, zt_done, h0_ready = (
            sem(n) for n in ("fin_done", "o_stat", "o_agg", "o_root", "o_recip", "z_ready",
                             "zt_done", "h0_ready"))
        h1_done, h1_ready, h2_done, h2_ready, h3_done, y_ready, stored = (
            sem(n) for n in ("h1_done", "h1_ready", "h2_done", "h2_ready", "h3_done", "y_ready",
                             "stored"))

        def wait(eng, s, value):
            if not isinstance(value, int) or value > 0:
                eng.wait_ge(s, value)

        block = ctx.enter_context(nc.Block())

        @block.sync
        def _(sp):
            sp.dma_start(ids[:, :], a["ids"]).then_inc(ids_in, 16)
            sp.dma_start(base[:, :], a["base"]).then_inc(ids_in, 16)
            for dst, name in ((ws[:, :], "ws"), (center[:, :], "center"), (gs[:, :], "gs"),
                              (ident[:, :], "ident"), (wsi[:, :, :], "wsi"),
                              (touch[:, :, :], "touch")):
                sp.dma_start(dst, a[name]).then_inc(early_in, 16)
            for dst, name in ((dense_t[:, :, :], "dense_t"), (wd[:, :, :], "wd"), (gdb[:, :], "gdb")):
                sp.dma_start(dst, a[name]).then_inc(x_in, 16)
            for dst, name in ((wsi9[:, :, :], "wsi9"), (bs9[:, :], "bs9"), (part9[:, :], "part9")):
                sp.dma_start(dst, a[name]).then_inc(bias_in, 16)
            for dst, name in ((wl[:, :, :], "wl"), (fold[:, :], "fold"), (row_scale[:, :], "row_scale"),
                              (is_row[:, :], "is_row"), (is_col[:, :, :], "is_col"),
                              (is_x[:, :], "is_x")):
                sp.dma_start(dst, a[name]).then_inc(wl_in, 16)
            for dst, name in ((glb[:, :, :], "glb"), (w1[:, :, :], "w1"), (b1[:, :], "b1"),
                              (w2[:, :, :], "w2"), (b2[:, :], "b2"), (w3[:, :], "w3")):
                sp.dma_start(dst, a[name]).then_inc(mlp_in, 16)
            sp.wait_ge(y_ready, TILES)
            sp.dma_start(out, y_row[:, :]).then_inc(stored, 16)
            sp.wait_ge(stored, 16)

        @block.gpsimd
        def _(pool):
            pool.wait_ge(ids_in, 32)
            pool.tensor_tensor(
                index[:, :].rearrange("p (k s) -> p k s", k=TILES),
                ids[:, :].rearrange("p (k s) -> p k s", k=TILES),
                base[:, :].unsqueeze(1).to_broadcast([P, TILES, 2 * PAIRS]), ALU.add,
            ).then_inc(index_ready, 1)
            pool.wait_ge(index_ready, 1)
            for k in range(TILES):
                for c in range(CHUNKS):
                    wait(pool, u_done, CHUNKS * (k - 1) + c + 1)
                    for s in chunk_pairs(c):
                        for t in (2 * s, 2 * s + 1):
                            at = 2 * PAIRS * k + t
                            pool.indirect_dma_start(
                                e[:, t, :], None, a["table"],
                                bass.IndirectOffsetOnAxis(ap=index[:, at:at + 1], axis=0),
                            ).then_inc(gathered[c], 16)

        @block.tensor
        def _(pe):
            def transposes(k, c):
                wait(pe, gathered[c], 16 * 2 * len(chunk_pairs(c)) * (k + 1))
                wait(pe, et_copied, CHUNKS * k + c)
                for n, s in enumerate(chunk_pairs(c)):
                    last = pe.transpose(p_tr[:, n * P:(n + 1) * P],
                                        e[:, 2 * s:2 * s + 2, :].rearrange("p h d -> p (h d)"),
                                        ident[:, :])
                last.then_inc(tr_done, 1)

            def e_gram(k, c):
                q = CHUNKS * k + c
                wait(pe, et_copied, q + 1)
                wait(pe, prod_done, q)
                for n, s in enumerate(chunk_pairs(c)):
                    last = pe.matmul(p_eg[:, n * P:(n + 1) * P], e_t[:, c % 2, n * P:(n + 1) * P],
                                     gram_w[:, :], start=True, stop=True)
                last.then_inc(eg_done, 1)

            def fields(k, c):
                q = CHUNKS * k + c
                wait(pe, e_scaled, q + 1)
                wait(pe, u_copied, q - 1)
                for s in chunk_pairs(c):
                    lo, hi = touched(s)
                    for bk in range(lo // CB, hi // CB + 1):
                        b0, b1_ = max(lo, bk * CB), min(hi, bk * CB + CB - 1)
                        if bk > c:
                            wait(pe, u_copied, q)
                        for h in range(2):
                            last = pe.matmul(
                                p_u[bk % 2][HALF * h:HALF * h + HALF,
                                            (b0 - bk * CB) * PROJ:(b1_ + 1 - bk * CB) * PROJ],
                                e[:, 2 * s + h, :],
                                wt[:, s, b0 - lo:b1_ + 1 - lo, :].rearrange("p b j -> p (b j)"),
                                start=b0 == bk * CB and P * s <= bk * CB * FIELDS,
                                stop=b1_ == bk * CB + CB - 1, skip_group_check=True)
                last.then_inc(u_done, 1)

            def project(k, c):
                q = CHUNKS * k + c
                for h in range(2):
                    wait(pe, y_normed, 2 * (q - 1) + h + 1)
                    pe.matmul(p_y[h][:, :], bias_l[:, :],
                              bias_r[:, :, :].rearrange("p b j -> p (b j)"), start=True, stop=False)
                    if h == 0:
                        wait(pe, u_copied, q + 1)
                    pe.matmul(p_y[h][:, :], wg_half[:, h, :], u[:, c % 2, :], start=False,
                              stop=True).then_inc(y_done, 1)

            def sample_gram(k, c):
                q = CHUNKS * k + c
                wait(pe, y_normed, 2 * q + 2)
                wait(pe, x_placed, q + 1)
                wait(pe, gr_copied, q)
                for h in range(2):
                    for g in range(CG):
                        at = (h * CG + g) * ITEM
                        for b in range(4):
                            it = items[:, c, h, 4 * g + b, :]
                            last = pe.matmul(p_gr[PROJ * b:PROJ * b + PROJ, at:at + PROJ + 1],
                                             it[:, 2:ITEM], it[:, 0:PROJ + 1], start=True, stop=True)
                last.then_inc(gr_done, 1)

            def interact(k):
                wait(pe, moved, k + 1)
                wait(pe, sumx_placed, k + 1)
                wait(pe, y_ready, k)
                for j in range(JX):
                    pe.matmul(p_o[:, :], z_q[:, j, :], we[:, j, :], start=(j == 0), stop=False)
                pe.matmul(p_o[:, :], z_x[:, :], wx[:, :], start=False, stop=True).then_inc(fin_done, 1)

            def turn_z(k):
                wait(pe, z_ready, k + 1)
                for n in range(KEPT // P):
                    last = pe.transpose(p_o[:, n * P:(n + 1) * P], z[:, n * P:(n + 1) * P], ident[:, :])
                last.then_inc(zt_done, 1)

            def hidden1(k):
                wait(pe, h0_ready, k + 1)
                nz, nd = KEPT // P, DENSE // P
                for m in range(HID1 // P):
                    for n in range(nz + nd):
                        rhs = h0[:, n, :] if n < nz else dense_t[:, n - nz, bass.ds(k * P, P)]
                        last = pe.matmul(p_o[:, m * P:(m + 1) * P], w1[:, n, m * P:(m + 1) * P], rhs,
                                         start=(n == 0), stop=(n == nz + nd - 1))
                last.then_inc(h1_done, 1)

            def hidden2(k):
                wait(pe, h1_ready, k + 1)
                for m in range(HID2 // P):
                    for n in range(HID1 // P):
                        last = pe.matmul(p_o[:, m * P:(m + 1) * P], w2[:, n, m * P:(m + 1) * P],
                                         h1[:, n, :], start=(n == 0), stop=(n == HID1 // P - 1))
                last.then_inc(h2_done, 1)

            def result(k):
                wait(pe, h2_ready, k + 1)
                for n in range(HID2 // P):
                    last = pe.matmul(p_o[0:1, 0:P], w3[:, n:n + 1], h2[:, n, :], start=(n == 0),
                                     stop=(n == HID2 // P - 1))
                last.then_inc(h3_done, 1)

            pe.wait_ge(early_in, 96)
            pe.matmul(p_o[:, 0:P], center[:, :], ws[:, :].unsqueeze(1).to_broadcast([EMB, 2, DIM]),
                      start=True, stop=True).then_inc(pe_wc, 1)
            pe.wait_ge(wc_ready, 1)
            pe.matmul(p_gr[:, 0:P], wc[:, :, :].rearrange("p h d -> p (h d)"),
                      wc[:, :, :].rearrange("p h d -> p (h d)"), start=True, stop=True).then_inc(pe_gram, 1)
            pe.wait_ge(wg_ready, 1)
            pe.transpose(p_o[:, 0:P], wg[:, :, :].rearrange("p h d -> p (h d)"),
                         ident[:, :]).then_inc(pe_wg, 1)
            pe.wait_ge(x_in, 48)
            for t in range(TILES):
                for n in range(2):
                    last = pe.matmul(p_y[0][:, t * EMB:(t + 1) * EMB], dense_t[:, n, t * P:(t + 1) * P],
                                     wd[:, n, :], start=(n == 0), stop=(n == 1))
            last.then_inc(pe_x, 1)
            pe.wait_ge(xn_ready, 1)
            for t in range(TILES):
                last = pe.transpose(p_y[1][:, t * P:(t + 1) * P], xn[:, t, :], ident[:, :])
            last.then_inc(pe_xt, 1)
            pe.wait_ge(xt_ready, 1)
            pe.wait_ge(ones_ready, 1)
            pe.wait_ge(half_ready, 1)
            pe.matmul(p_o[ROW_SUMX:ROW_SUMX + 1, :], ones[:, :], x_t[:, :], start=True,
                      stop=True).then_inc(pe_sumx, 1)
            pe.wait_ge(mix_ready, 1)
            pe.wait_ge(wl_in, 96)
            pe.wait_ge(gram_ready, 1)
            for j in range(JX):
                last = pe.matmul(p_gr[:, :], mix[:, j, :], wl[:, j, :], start=(j == 0), stop=(j == JX - 1))
            last.then_inc(pe_wx, 1)

            def tile(k, first):
                for c in range(CHUNKS):
                    if c == 2 and not first:
                        turn_z(k - 1)
                    if first and c == 0:
                        pe.wait_ge(gram_ready, 1)
                        pe.wait_ge(half_ready, 1)
                    e_gram(k, c)
                    if not (first and c == 0):
                        if first and c == 1:
                            pe.wait_ge(bias_ready, 1)
                        project(*before(k, c))
                    if not first:
                        if c == 1:
                            interact(k - 1)
                        if c == 2:
                            hidden1(k - 1)
                        if c == 3:
                            hidden2(k - 1)
                    if first and c == 0:
                        pe.wait_ge(wt_ready, 1)
                    fields(k, c)
                    if not first and c == 3:
                        result(k - 1)
                    if not (first and c == 0):
                        if first and c == 1:
                            pe.wait_ge(wx_ready, 1)
                            pe.wait_ge(items_one, 1)
                        sample_gram(*before(k, c))
                    if c < CHUNKS - 1:
                        transposes(k, c + 1)

            transposes(0, 0)
            tile(0, True)
            pe.wait_ge(mlp_in, 96)
            pe.wait_ge(we_ready, 1)
            with pe.Fori(1, TILES) as k:
                transposes(k, 0)
                tile(k, False)
            k = TILES - 1
            project(k, CHUNKS - 1)
            sample_gram(k, CHUNKS - 1)
            interact(k)
            turn_z(k)
            hidden1(k)
            hidden2(k)
            result(k)

        @block.vector
        def _(dve):
            count = [0]

            def link(ins):
                count[0] += 1
                ins.then_inc(dve_setup, 1)
                dve.wait_ge(dve_setup, count[0])

            def bcast(ap, n):
                return ap.unsqueeze(2).to_broadcast([ap.shape[0], ap.shape[1], n])

            dve.memset(eps[:, :], EPS).then_inc(eps_ready, 1)
            dve.memset(ones[:, :], 1.0).then_inc(ones_ready, 1)
            link(dve.memset(gram_w[:, :], 0.0))
            link(dve.memset(wg_half[:, :, :], 0.0))
            dve.wait_ge(early_in, 96)
            dve.wait_ge(pe_wc, 1)
            dve.tensor_copy(wc[:, :, :].rearrange("p h d -> p (h d)"), p_o[:, 0:P]).then_inc(wc_ready, 1)
            dve.tensor_scalar(wg[:, :, :].rearrange("p h d -> p (h d)"), p_o[:, 0:P], gs[:, 0:1], None,
                              ALU.mult).then_inc(wg_ready, 1)
            dve.wait_ge(pe_gram, 1)
            for h in range(2):
                r = slice(DIM * h, DIM * h + DIM)
                last = dve.tensor_copy(gram_w[r, r], p_gr[r, r])
            last.then_inc(gram_ready, 1)
            dve.wait_ge(pe_wg, 1)
            for h in range(2):
                r = slice(DIM * h, DIM * h + DIM)
                last = dve.tensor_copy(wg_half[r, h, :], p_o[r, 0:P])
            last.then_inc(half_ready, 1)
            link(dve.tensor_reduce(wsi_mean[:, :], wsi[:, :, :], AX_X, ALU.add))
            link(dve.tensor_scalar(wsi_mean[:, :], wsi_mean[:, :], 1.0 / PROJ, None, ALU.mult))
            link(dve.tensor_tensor(wsi[:, :, :], wsi[:, :, :], bcast(wsi_mean[:, :], PROJ), ALU.subtract))
            dve.tensor_tensor(
                wt[:, :, :, :], wsi[:, :, :].unsqueeze(2).to_broadcast([P, PAIRS, TOUCH, PROJ]),
                touch[:, :, :].unsqueeze(3).to_broadcast([P, PAIRS, TOUCH, PROJ]),
                ALU.mult).then_inc(wt_ready, 1)
            dve.wait_ge(pe_x, 1)
            for t in range(TILES):
                last = dve.bn_stats(x_stats[:, t, :], p_y[0][:, t * EMB:(t + 1) * EMB])
            link(last)
            for t in range(TILES):
                last = dve.bn_aggr(x_mv[:, t, :], x_stats[:, t, :])
            last.then_inc(x_agg, 1)
            dve.wait_ge(x_agg, 1)
            dve.wait_ge(x_root, 1)
            link(dve.reciprocal(x_rs[:, :], x_sd[:, :]))
            for t in range(TILES):
                last = dve.tensor_scalar(xn[:, t, :], p_y[0][:, t * EMB:(t + 1) * EMB],
                                         x_mv[:, t, 0:1], x_rs[:, t:t + 1], ALU.subtract, ALU.mult)
            last.then_inc(xn_ready, 1)
            link(dve.memset(bias_l[:, :], 0.0))
            link(dve.memset(bias_r[:, :, :], 0.0))
            dve.wait_ge(bias_in, 48)
            link(dve.tensor_reduce(wsum9[:, :], wsi9[:, :, :], AX_X, ALU.add))
            link(dve.tensor_reduce(wmean9[:, :], wsum9[:, :], AX_X, ALU.add))
            link(dve.tensor_scalar(wmean9[:, :], wmean9[:, :], 1.0 / PROJ, None, ALU.mult))
            link(dve.tensor_scalar(wsum9[:, :], wsum9[:, :], wmean9[:, 0:1], None, ALU.subtract))

            def parts(value, n, masks, dst):
                link(dve.tensor_copy(split_h[:, 0, 0:n], value))
                link(dve.tensor_tensor(split_r[:, 0, 0:n], value, split_h[:, 0, 0:n], ALU.subtract))
                link(dve.tensor_copy(split_h[:, 1, 0:n], split_r[:, 0, 0:n]))
                link(dve.tensor_tensor(split_r[:, 1, 0:n], split_r[:, 0, 0:n], split_h[:, 1, 0:n],
                                       ALU.subtract))
                link(dve.tensor_copy(split_h[:, 2, 0:n], split_r[:, 1, 0:n]))
                link(dve.tensor_scalar(split_t[:, 0, 0:n], split_h[:, 0, 0:n], part9[:, masks:masks + 1],
                                       None, ALU.mult))
                link(dve.scalar_tensor_tensor(split_t[:, 1, 0:n], split_h[:, 1, 0:n],
                                              part9[:, masks + 1:masks + 2], split_t[:, 0, 0:n],
                                              ALU.mult, ALU.add))
                link(dve.scalar_tensor_tensor(dst, split_h[:, 2, 0:n], part9[:, masks + 2:masks + 3],
                                              split_t[:, 1, 0:n], ALU.mult, ALU.add))

            parts(bs9[:, :], EMB, 0, bias_l[0:9, :])
            parts(wsum9[:, :], PROJ, PARTS, bias_w[:, :])
            dve.tensor_copy(bias_r[0:9, :, :],
                            bias_w[:, :].unsqueeze(1).to_broadcast([9, CB, PROJ])).then_inc(bias_ready, 1)
            dve.memset(items[:, :, :, :, 0:1], 1.0).then_inc(items_one, 1)
            link(dve.memset(z_x[:, :], 0.0))
            dve.memset(z_x[ROW_ONE:ROW_ONE + 1, :], 1.0).then_inc(zx_clear, 1)
            link(dve.memset(mix[:, :, :], 0.0))
            dve.wait_ge(wl_in, 96)
            g_i, b_i = fold[:, 0:1], fold[:, 1:2]
            g_c, b_c = fold[:, 2:2 + JX], fold[:, 2 + JX:2 + 2 * JX]
            dve.tensor_scalar(scale_w[:, :], g_c, g_i, None, ALU.mult).then_inc(scale_ready, 1)
            dve.tensor_scalar(mix[:, :, 0:PROJ], is_col[:, :, :], b_i, None, ALU.mult)
            link(dve.tensor_tensor(mix_t[:, :, :], is_row[:, :].unsqueeze(1).to_broadcast([P, JX, PROJ]),
                                   bcast(b_c, PROJ), ALU.mult))
            link(dve.tensor_tensor(mix[:, :, 0:PROJ], mix[:, :, 0:PROJ], mix_t[:, :, :], ALU.add))
            dve.tensor_scalar(mix[:, :, ROW_SUMX], is_x[:, :], b_i, None, ALU.mult)
            dve.tensor_scalar(mix[:, :, ROW_ONE], b_c, b_i, float(EMB), ALU.mult,
                              ALU.mult).then_inc(mix_ready, 1)

            def rows(k, c):
                q = CHUNKS * k + c
                pairs = chunk_pairs(c)
                n, at = 2 * len(pairs), 2 * pairs[0]
                dve.wait_ge(eg_done, q + 1)
                mine = e[:, at:at + n, :]
                dve.tensor_tensor(prod[:, 0:n * DIM], mine.rearrange("p t d -> p (t d)"),
                                  p_eg[:, 0:n * DIM], ALU.mult).then_inc(prod_done, 1)
                dve.wait_ge(prod_done, q + 1)
                dve.tensor_reduce(ss[:, 0:n], prod[:, 0:n * DIM].rearrange("p (t d) -> p t d", d=DIM),
                                  AX_X, ALU.add).then_inc(ss_done, 1)
                dve.wait_ge(ss_done, q + 1)
                dve.tensor_scalar(var[:, 0:n], ss[:, 0:n], 1.0 / EMB, 0.0, ALU.mult,
                                  ALU.max).then_inc(var_done, 1)
                dve.wait_ge(sd_done, q + 1)
                dve.reciprocal(rs[:, 0:n], sd[:, 0:n]).then_inc(rs_done, 1)
                dve.wait_ge(rs_done, q + 1)
                dve.tensor_tensor(mine, mine, bcast(rs[:, 0:n], DIM), ALU.mult).then_inc(e_scaled, 1)

            def norm(k, c):
                q = CHUNKS * k + c
                for h in range(2):
                    dve.wait_ge(sq_done, 2 * q + h + 1)
                    dve.tensor_reduce(ss2[:, h, :], sq[:, h, :].rearrange("p (b j) -> p b j", j=PROJ),
                                      AX_X, ALU.add).then_inc(ss2_done, 1)
                for h in range(2):
                    dve.wait_ge(sd2_done, 2 * q + h + 1)
                    dve.reciprocal(rs2[:, h, :], sd2[:, h, :]).then_inc(rs2_done, 1)
                wait(dve, gr_done, q - CHUNKS + 1)
                for h in range(2):
                    dve.wait_ge(rs2_done, 2 * q + h + 1)
                    dve.tensor_tensor(items[:, c, h, :, 2:ITEM],
                                      p_y[h][:, :].rearrange("p (b j) -> p b j", j=PROJ),
                                      bcast(rs2[:, h, :], PROJ), ALU.mult).then_inc(y_normed, 1)

            def move(k):
                dve.wait_ge(gr_copied, CHUNKS * k + CHUNKS)
                wait(dve, fin_done, k)
                for b in range(4):
                    src = slice(PROJ * b, PROJ * b + PROJ)
                    for jj in range(4):
                        dve.tensor_copy(
                            z_q[PROJ * jj:PROJ * jj + PROJ, :, b::4].rearrange("p j g -> p g j"),
                            z_s[src, :, 1 + JX * jj:1 + JX * jj + JX])
                    last = dve.tensor_copy(z_x[0:PROJ, b::4], z_s[src, :, 0])
                last.then_inc(moved, 1)

            def out_norm(k):
                dve.wait_ge(fin_done, k + 1)
                dve.bn_stats(o_stats[:, :], p_o[:, :]).then_inc(o_stat, 1)
                dve.drain()
                dve.bn_aggr(o_mv[:, :], o_stats[:, :]).then_inc(o_agg, 1)
                dve.wait_ge(o_root, k + 1)
                dve.reciprocal(o_rs[:, :], o_sd[:, :]).then_inc(o_recip, 1)
                dve.wait_ge(o_recip, k + 1)
                dve.tensor_scalar(z[:, :], p_o[:, 0:KEPT], o_mv[:, 0:1], o_rs[:, 0:1], ALU.subtract,
                                  ALU.mult).then_inc(z_ready, 1)

            def tile(k, first):
                for c in range(CHUNKS):
                    rows(k, c)
                    if not (first and c == 0):
                        norm(*before(k, c))
                    if c == 0 and not first:
                        move(k - 1)
                    if c == 1 and not first:
                        out_norm(k - 1)

            tile(0, True)
            with dve.Fori(1, TILES) as k:
                tile(k, False)
            norm(TILES - 1, CHUNKS - 1)
            move(TILES - 1)
            out_norm(TILES - 1)

        @block.scalar
        def _(act):
            def root(dst, src, scale):
                return act.activation(dst, src, ACT.Sqrt, bias=eps[0:dst.shape[0], 0:1], scale=scale)

            def copy_et(k, c):
                q = CHUNKS * k + c
                n = len(chunk_pairs(c)) * P
                act.wait_ge(tr_done, q + 1)
                wait(act, eg_done, q - 1)
                act.activation(e_t[:, c % 2, 0:n], p_tr[:, 0:n], ACT.Copy).then_inc(et_copied, 1)

            def row_root(k, c):
                q = CHUNKS * k + c
                n = 2 * len(chunk_pairs(c))
                act.wait_ge(var_done, q + 1)
                wait(act, rs_done, q)
                root(sd[:, 0:n], var[:, 0:n], 1.0).then_inc(sd_done, 1)

            def squares(k, c):
                q = CHUNKS * k + c
                for h in range(2):
                    act.wait_ge(y_done, 2 * q + h + 1)
                    wait(act, ss2_done, 2 * (q - 1) + h + 1)
                    act.activation(sq[:, h, :], p_y[h][:, :], ACT.Square).then_inc(sq_done, 1)
                for h in range(2):
                    act.wait_ge(ss2_done, 2 * q + h + 1)
                    wait(act, rs2_done, 2 * (q - 1) + h + 1)
                    root(sd2[:, h, :], ss2[:, h, :], 1.0 / PROJ).then_inc(sd2_done, 1)

            def place_x(k, c):
                q = CHUNKS * k + c
                wait(act, gr_done, q - CHUNKS + 1)
                for h in range(2):
                    last = act.activation(items[:, c, h, :, 1],
                                          x_t[:, bass.ds(k * P + (HALF * h + CB * c), CB)], ACT.Copy)
                last.then_inc(x_placed, 1)

            def copy_u(k, c):
                q = CHUNKS * k + c
                act.wait_ge(u_done, q + 1)
                wait(act, y_done, 2 * (q - 1))
                act.activation(u[:, c % 2, :], p_u[c % 2][:, :], ACT.Copy).then_inc(u_copied, 1)

            def copy_gram(k, c):
                act.wait_ge(gr_done, CHUNKS * k + c + 1)
                wait(act, moved, k)
                per_half = GROUPS // 2
                for h in range(2):
                    at = per_half * h + CG * c
                    last = act.activation(
                        z_s[:, at:at + CG, 0:PROJ + 1],
                        p_gr[:, h * CG * ITEM:(h + 1) * CG * ITEM]
                        .rearrange("p (g j) -> p g j", j=ITEM)[:, :, 0:PROJ + 1], ACT.Copy)
                last.then_inc(gr_copied, 1)

            def place_sumx(k):
                wait(act, fin_done, k)
                act.activation(z_x[ROW_SUMX:ROW_SUMX + 1, :],
                               sumx[ROW_SUMX:ROW_SUMX + 1, bass.ds(k * P, P)],
                               ACT.Copy).then_inc(sumx_placed, 1)

            def out_root(k):
                act.wait_ge(o_agg, k + 1)
                root(o_sd[:, :], o_mv[:, 1:2], 1.0).then_inc(o_root, 1)

            def gain_z(k):
                act.wait_ge(zt_done, k + 1)
                wait(act, h1_done, k)
                for n in range(KEPT // P):
                    last = act.activation(h0[:, n, :], p_o[:, n * P:(n + 1) * P], ACT.Identity,
                                          bias=glb[:, 1, n:n + 1], scale=glb[:, 0, n:n + 1])
                last.then_inc(h0_ready, 1)

            def relu1(k):
                act.wait_ge(h1_done, k + 1)
                wait(act, h2_done, k)
                for n in range(HID1 // P):
                    last = act.activation(h1[:, n, :], p_o[:, n * P:(n + 1) * P], ACT.Relu,
                                          bias=b1[:, n:n + 1])
                last.then_inc(h1_ready, 1)

            def relu2(k):
                act.wait_ge(h2_done, k + 1)
                wait(act, h3_done, k)
                for n in range(HID2 // P):
                    last = act.activation(h2[:, n, :], p_o[:, n * P:(n + 1) * P], ACT.Relu,
                                          bias=b2[:, n:n + 1])
                last.then_inc(h2_ready, 1)

            def copy_y(k):
                act.wait_ge(h3_done, k + 1)
                act.activation(y_row[:, bass.ds(k * P, P)], p_o[0:1, 0:P], ACT.Copy).then_inc(y_ready, 1)

            act.wait_ge(eps_ready, 1)
            act.wait_ge(x_agg, 1)
            root(x_sd[:, :], x_mv[:, :, 1], 1.0).then_inc(x_root, 1)
            act.wait_ge(pe_xt, 1)
            act.wait_ge(x_in, 48)
            act.activation(x_t[:, :], p_y[1][:, :], ACT.Identity, bias=gdb[:, 1:2],
                           scale=gdb[:, 0:1]).then_inc(xt_ready, 1)
            act.wait_ge(pe_sumx, 1)
            act.activation(sumx[ROW_SUMX:ROW_SUMX + 1, :], p_o[ROW_SUMX:ROW_SUMX + 1, :],
                           ACT.Copy).then_inc(sumx_ready, 1)
            act.wait_ge(sumx_ready, 1)
            act.wait_ge(xt_ready, 1)
            act.wait_ge(scale_ready, 1)
            act.wait_ge(wl_in, 96)
            for j in range(JX):
                last = act.activation(we[:, j, :], wl[:, j, :], ACT.Copy, scale=scale_w[:, j:j + 1])
            last.then_inc(we_ready, 1)
            act.wait_ge(pe_wx, 1)
            act.activation(wx[:, :], p_gr[:, :], ACT.Copy, scale=row_scale[:, 0:1]).then_inc(wx_ready, 1)

            def tile(k, first):
                for c in range(CHUNKS):
                    row_root(k, c)
                    if c == 2 and not first:
                        gain_z(k - 1)
                    if not (first and c == 0):
                        squares(*before(k, c))
                    place_x(k, c)
                    if not first:
                        if c == 0:
                            place_sumx(k - 1)
                        if c == 1:
                            out_root(k - 1)
                        if c == 2:
                            relu1(k - 1)
                        if c == 3:
                            relu2(k - 1)
                    copy_u(k, c)
                    if not first and c == 3:
                        copy_y(k - 1)
                    if not (first and c == 0):
                        copy_gram(*before(k, c))
                    if c < CHUNKS - 1:
                        copy_et(k, c + 1)

            copy_et(0, 0)
            tile(0, True)
            act.wait_ge(zx_clear, 1)
            act.wait_ge(mlp_in, 96)
            with act.Fori(1, TILES) as k:
                copy_et(k, 0)
                tile(k, False)
            k = TILES - 1
            squares(k, CHUNKS - 1)
            copy_gram(k, CHUNKS - 1)
            place_sumx(k)
            out_root(k)
            gain_z(k)
            relu1(k)
            relu2(k)
            copy_y(k)


def before(k, c):
    return (k, c - 1) if c else (k - 1, CHUNKS - 1)


def kernel(**inputs):
    import numpy as np
    import concourse.bacc as bacc
    from concourse.bass_utils import run_bass_kernel_spmd

    def arr(name):
        return np.asarray(inputs[name])

    tables = [arr(f"tbl_{f}") for f in range(FIELDS)]
    starts = np.concatenate([[0], np.cumsum([t.shape[0] for t in tables])[:-1]]).astype(np.int32)
    rows = np.arange(PAIRS * P).reshape(PAIRS, P)
    field, sample = rows % FIELDS, rows // FIELDS
    part = np.arange(P)
    row_i, quad = part % PROJ, part // PROJ
    col = JX * quad[:, None] + np.arange(JX)[None, :]
    valid = col <= row_i[:, None]
    flat = np.where(valid, (row_i[:, None] + 1) * row_i[:, None] // 2 + col, 0)
    wl_t = arr("L0_rec_Wl").T
    gsi, bsi = arr("L0_rec_gsi"), arr("L0_rec_bsi")
    wsi_a = arr("L0_rec_Wsi")
    r9 = np.arange(9)
    pick = np.concatenate([r9[:, None] // PARTS == np.arange(PARTS), r9[:, None] % PARTS == np.arange(PARTS)], 1)
    rest = np.ones(P - PROJ, np.float32)
    f32 = np.float32

    def split_rows(w, n):
        return w.reshape(n, P, -1).transpose(1, 0, 2)

    arrays = {
        "table": np.concatenate(tables, 0),
        "ids": arr("ids").reshape(TILES, 2, PAIRS, P).transpose(3, 0, 2, 1).reshape(P, -1),
        "base": np.repeat(starts[field.T], 2, 1),
        "ws": arr("L0_rec_Ws"),
        "center": (np.eye(P) - 1.0 / P).astype(f32),
        "gs": arr("L0_rec_gs")[:, None],
        "ident": np.eye(P, dtype=f32),
        "wsi": wsi_a.T[field].transpose(1, 0, 2),
        "touch": (sample.T[:, :, None] - (P * np.arange(PAIRS) // FIELDS)[None, :, None]
                  == np.arange(TOUCH)).astype(f32),
        "dense_t": split_rows(arr("r_dense_t").T, 2),
        "wd": split_rows(arr("L0_rec_Wd").T, 2),
        "gdb": np.stack([arr("L0_rec_gd"), arr("L0_rec_bd")], 1),
        "wsi9": np.stack([wsi_a] * 9),
        "bs9": np.stack([arr("L0_rec_bs")] * 9),
        "part9": pick.astype(f32),
        "wl": np.where(valid[:, :, None], wl_t[flat], f32(0)),
        "fold": np.concatenate([
            gsi[row_i][:, None], bsi[row_i][:, None],
            np.where(col > 0, gsi[np.maximum(col - 1, 0)], f32(1)),
            np.where(col > 0, bsi[np.maximum(col - 1, 0)], f32(0))], 1),
        "row_scale": np.concatenate([gsi, rest])[:, None],
        "is_row": (row_i[:, None] == np.arange(PROJ)).astype(f32),
        "is_col": (col[:, :, None] - 1 == np.arange(PROJ)).astype(f32),
        "is_x": (col == 0).astype(f32),
        "glb": np.stack([arr("L0_rec_gl")[:KEPT].reshape(-1, P).T, arr("L0_rec_bl")[:KEPT].reshape(-1, P).T], 1),
        "w1": split_rows(np.concatenate([arr("W_top1")[:KEPT], arr("W_top1")[MAXD:]]), (KEPT + DENSE) // P),
        "b1": arr("b_top1").reshape(-1, P).T,
        "w2": split_rows(arr("W_top2"), HID1 // P),
        "b2": arr("b_top2").reshape(-1, P).T,
        "w3": arr("W_top3").reshape(-1, P).T,
    }
    arrays = {name: np.ascontiguousarray(x) for name, x in arrays.items()}

    nc = bacc.Bacc("TRN2", target_bir_lowering=False, num_devices=1)
    aps = {name: nc.dram_tensor(f"in_{name}", x.shape, mybir.dt.from_np(x.dtype), kind="ExternalInput").ap()
           for name, x in arrays.items()}
    out = nc.dram_tensor("out_y", (1, BATCH), F32, kind="ExternalOutput").ap()
    build(nc, aps, out)
    r = run_bass_kernel_spmd(nc, [{f"in_{name}": x for name, x in arrays.items()}], core_ids=[0])
    return r.results[0]["out_y"].reshape(BATCH, 1)
```

```python
from contextlib import ExitStack

import concourse.bass as bass
from concourse import mybir

F32 = mybir.dt.float32
F32R = mybir.dt.float32r
I32 = mybir.dt.int32
ALU = mybir.AluOpType
ACT = mybir.ActivationFunctionType
AX_X = mybir.AxisListType.X

P = 128
BATCH = 512
FIELDS = 26
DIM = 64
EMB = 128
PROJ = 32
DENSE = 256
MAXD = 512
KEPT = 384
HID1, HID2 = 512, 256
EPS = 1e-5

TILES = BATCH // P
HALF = P // 2
PAIRS = HALF * FIELDS // P
CHUNKS = 4
CB = HALF // CHUNKS
BANK = CB * PROJ
TOUCH = 6
ITEM = PROJ + 2
GROUPS = P // 4
CG = CB // 4
BLOCKS = PROJ // 2
JX = BLOCKS // 4
KX = JX + 1
DENSE_BANKS = 3
ROW_SUMX, ROW_X, ROW_ONE = 32, 64, 96
PARTS = 2


def chunk_pairs(c):
    last = [((c1 + 1) * CB * FIELDS - 1) // P for c1 in range(CHUNKS)]
    return range(0 if c == 0 else last[c - 1] + 1, last[c] + 1)


def touched(s):
    return P * s // FIELDS, (P * s + P - 1) // FIELDS


Z_PARTS = (range(0, KX // 2), range(KX // 2, KX))
MOST = max(len(chunk_pairs(c)) for c in range(CHUNKS))


def build(nc, a, out):
    with ExitStack() as ctx:
        def sb(name, shape, dt=F32):
            return ctx.enter_context(nc.sbuf_tensor(name, shape, dt))

        def bank(name):
            return ctx.enter_context(nc.psum_tensor(name, [P, 512], F32))

        def sem(name):
            return ctx.enter_context(nc.semaphore(name))

        rows_in = sb("rows_in", [P, (TILES + 2) * 2 * PAIRS], I32)
        base, ids = rows_in[:, 0:2 * PAIRS], rows_in[:, 2 * PAIRS:]
        index = sb("index", [P, 2 * PAIRS], I32)
        setup = sb("setup", [P, 2 * P + DIM + 1])
        ident, center = setup[:, 0:P], setup[:, P:2 * P]
        ws, gs = setup[:, 2 * P:2 * P + DIM], setup[:, 2 * P + DIM:]
        wc = sb("wc", [EMB, 2, DIM])
        wg = sb("wg", [EMB, 2, DIM])
        gram_w = sb("gram_w", [P, P])
        wg_hi = sb("wg_hi", [P, 2, EMB], F32R)
        wg_lo = sb("wg_lo", [P, 2, EMB], F32R)
        wsi_touch = sb("wsi_touch", [P, PAIRS, PROJ + TOUCH])
        wsi, touch = wsi_touch[:, :, 0:PROJ], wsi_touch[:, :, PROJ:]
        wsi_mean = sb("wsi_mean", [P, PAIRS])
        wt = sb("wt", [P, PAIRS, TOUCH, PROJ])
        bias4 = sb("bias4", [PARTS ** 2, PROJ * FIELDS + EMB + 2 * PARTS])
        wsi4 = bias4[:, 0:PROJ * FIELDS].rearrange("p (j f) -> p j f", f=FIELDS)
        bs4 = bias4[:, PROJ * FIELDS:PROJ * FIELDS + EMB]
        part4 = bias4[:, PROJ * FIELDS + EMB:]
        wsum4 = sb("wsum4", [PARTS ** 2, PROJ])
        wmean4 = sb("wmean4", [PARTS ** 2, 1])
        split_h = sb("split_h", [PARTS ** 2, EMB], F32R)
        split_r = sb("split_r", [PARTS ** 2, EMB])
        split_t = sb("split_t", [PARTS ** 2, EMB])
        bias_w = sb("bias_w", [PARTS ** 2, PROJ])
        bias_l = sb("bias_l", [P, EMB], F32R)
        bias_r = sb("bias_r", [P, CB, PROJ], F32R)
        dense_wd = sb("dense_wd", [P, 2, BATCH + EMB + 1])
        dense_t, wd = dense_wd[:, :, 0:BATCH], dense_wd[:, :, BATCH:BATCH + EMB]
        gdb = dense_wd[:, :, BATCH + EMB]
        x_stats = sb("x_stats", [P, TILES, 6])
        x_mv = sb("x_mv", [P, TILES, 2])
        x_sd = sb("x_sd", [P, TILES])
        x_rs = sb("x_rs", [P, TILES])
        xn = sb("xn", [P, TILES, EMB])
        x_t = sb("x_t", [EMB, BATCH])
        ones = sb("ones", [P, 1])
        eps = sb("eps", [P, 1])
        warm = sb("warm", [P, 1])
        sumx = sb("sumx", [P, BATCH])
        wl = sb("wl", [P, KX, MAXD])
        we_hi = sb("we_hi", [P, KX, MAXD], F32R)
        we_lo = sb("we_lo", [P, KX, MAXD], F32R)
        fold = sb("fold", [P, 3 + 2 * JX + PROJ * (1 + JX)])
        g_i, b_i, row_scale = fold[:, 0:1], fold[:, 1:2], fold[:, 2:3]
        g_c, b_c = fold[:, 3:3 + JX], fold[:, 3 + JX:3 + 2 * JX]
        is_row = fold[:, 3 + 2 * JX:3 + 2 * JX + PROJ]
        is_col = fold[:, 3 + 2 * JX + PROJ:].rearrange("p (j n) -> p j n", n=PROJ)
        second = sb("second", [P, BLOCKS], I32)
        scale_w = sb("scale_w", [P, JX])
        mix = sb("mix", [P, KX, P])
        mix_t = sb("mix_t", [P, JX, PROJ])
        biases = sb("biases", [P, HID1 // P + HID2 // P + 2 * KEPT // P])
        b1, b2 = biases[:, 0:HID1 // P], biases[:, HID1 // P:HID1 // P + HID2 // P]
        glb = biases[:, HID1 // P + HID2 // P:].rearrange("p (g n) -> p g n", g=2)
        w1 = sb("w1", [P, KEPT // P, HID1])
        w1_dense = sb("w1_dense", [P, DENSE // P, HID1])
        d1 = sb("d1", [P, HID1 // P, BATCH])
        w2_w3 = sb("w2_w3", [P, HID1 // P * HID2 + HID2 // P])
        w2 = w2_w3[:, 0:HID1 // P * HID2].rearrange("p (n m) -> p n m", m=HID2)
        w3 = w2_w3[:, HID1 // P * HID2:]

        e = sb("e", [P, 2 * PAIRS, DIM])
        e_t = sb("e_t", [P, 2, MOST * P])
        prod = sb("prod", [P, MOST * P])
        ss = sb("ss", [P, 2 * MOST])
        var = sb("var", [P, 2 * MOST])
        sd = sb("sd", [P, 2 * MOST])
        rs = sb("rs", [P, 2 * MOST])
        u_hi = sb("u_hi", [P, 2, BANK], F32R)
        u_lo = sb("u_lo", [P, 2, BANK], F32R)
        sq = sb("sq", [P, 2, BANK])
        ss2 = sb("ss2", [P, 2, CB])
        sd2 = sb("sd2", [P, 2, CB])
        rs2 = sb("rs2", [P, 2, CB])
        items = sb("items", [EMB, CHUNKS, 2, CB, ITEM])
        z_s = sb("z_s", [P, GROUPS, ITEM])
        z_q = sb("z_q", [P, KX, P])
        z_hi = sb("z_hi", [P, KX, P], F32R)
        z_lo = sb("z_lo", [P, KX, P], F32R)
        o_stats = sb("o_stats", [P, 6])
        o_mv = sb("o_mv", [P, 2])
        o_sd = sb("o_sd", [P, 1])
        o_rs = sb("o_rs", [P, 1])
        z = sb("z", [P, KEPT])
        h0 = sb("h0", [P, KEPT // P, P])
        h1_sum = sb("h1_sum", [P, HID1 // P, P])
        h1 = sb("h1", [P, HID1 // P, P])
        h2 = sb("h2", [P, HID2 // P, BATCH])
        y_row = sb("y_row", [1, BATCH])

        p_tr, p_eg, p_gr, p_o = bank("p_tr"), bank("p_eg"), bank("p_gr"), bank("p_o")
        p_u = [bank("p_u0"), bank("p_u1")]
        p_y = [bank("p_y0"), bank("p_y1")]
        p_d = [p_y[0], p_y[1], p_gr]

        ids_in, ws_in, wsi_in, x_in, w1_in, bias_in, wl_in, mlp_in = (
            sem(n) for n in ("ids_in", "ws_in", "wsi_in", "x_in", "w1_in", "bias_in", "wl_in", "mlp_in"))
        gathered = [sem(f"gathered{c}") for c in range(CHUNKS)]
        index_ready, dve_setup = sem("index_ready"), sem("dve_setup")
        pe_wc, pe_gram, pe_wg = sem("pe_wc"), sem("pe_gram"), sem("pe_wg")
        wc_ready, wg_ready, gram_ready, half_ready = (
            sem(n) for n in ("wc_ready", "wg_ready", "gram_ready", "half_ready"))
        wt_ready, bias_ready, mix_ready, ones_ready, eps_ready = (
            sem(n) for n in ("wt_ready", "bias_ready", "mix_ready", "ones_ready", "eps_ready"))
        cleared, items_one, zx_clear = sem("cleared"), sem("items_one"), sem("zx_clear")
        pe_x, x_agg, x_root, xn_ready, pe_xt, xt_ready, pe_sumx, sumx_ready, pe_d1, d1_ready = (
            sem(n) for n in ("pe_x", "x_agg", "x_root", "xn_ready", "pe_xt", "xt_ready",
                             "pe_sumx", "sumx_ready", "pe_d1", "d1_ready"))
        pe_wx, scale_ready, we_hi_ready, wx_hi_ready, we_ready = (
            sem(n) for n in ("pe_wx", "scale_ready", "we_hi_ready", "wx_hi_ready", "we_ready"))
        tr_done, et_copied, eg_done, prod_done, ss_done, var_done, sd_done, rs_done, e_scaled = (
            sem(n) for n in ("tr_done", "et_copied", "eg_done", "prod_done", "ss_done", "var_done",
                             "sd_done", "rs_done", "e_scaled"))
        u_done, u_high, u_split, y_done, sq_done, ss2_done, sd2_done, rs2_done, y_normed = (
            sem(n) for n in ("u_done", "u_high", "u_split", "y_done", "sq_done", "ss2_done",
                             "sd2_done", "rs2_done", "y_normed"))
        x_placed, gr_done, gr_copied, merged, moved_dve, moved_act, z_high, z_split = (
            sem(n) for n in ("x_placed", "gr_done", "gr_copied", "merged", "moved_dve", "moved_act", "z_high",
                             "z_split"))
        fin_done, o_agg, o_root, o_recip, z_ready, zt_done, h0_ready = (
            sem(n) for n in ("fin_done", "o_agg", "o_root", "o_recip", "z_ready", "zt_done",
                             "h0_ready"))
        h1_done, h1_added, h1_ready, h2_done, h2_ready, y_done_pe, y_ready, stored = (
            sem(n) for n in ("h1_done", "h1_added", "h1_ready", "h2_done", "h2_ready", "y_done_pe",
                             "y_ready", "stored"))

        def wait(eng, s, value):
            if not isinstance(value, int) or value > 0:
                eng.wait_ge(s, value)

        def move_columns(copy, b, jj):
            return copy(z_q[PROJ * jj:PROJ * jj + PROJ, 0:JX, b::4].rearrange("p j g -> p g j"),
                        z_s[PROJ * b:PROJ * b + PROJ, :, 2 + JX * jj:2 + JX * jj + JX])

        block = ctx.enter_context(nc.Block())

        @block.sync
        def _(sp):
            def load(signal, *what):
                for dst, name in what:
                    sp.dma_start(dst, a[name]).then_inc(signal, 16)

            load(ids_in, (rows_in[:, :], "rows_in"))
            load(x_in, (dense_wd[:, :, :], "dense_wd"))
            load(w1_in, (w1_dense[:, :, :], "w1_dense"), (biases[:, :], "biases"))
            sp.wait_ge(gathered[0], 16 * 2 * len(chunk_pairs(0)))
            load(wl_in, (fold[:, :], "fold"), (second[:, :], "second"), (wl[:, :, :], "wl"))
            sp.wait_ge(gathered[2], 16 * 2 * len(chunk_pairs(2)))
            load(mlp_in, (w1[:, :, :], "w1"), (w2_w3[:, :], "w2_w3"))
            sp.wait_ge(y_ready, 2)
            sp.dma_start(out, y_row[:, :]).then_inc(stored, 16)
            sp.wait_ge(stored, 16)

        @block.gpsimd
        def _(pool):
            pool.memset(mix[:, :, :], 0.0).then_inc(cleared, 1)
            pool.memset(bias_l[:, :].bitcast(F32), 0.0).then_inc(cleared, 1)
            pool.memset(bias_r[:, :, :].bitcast(F32), 0.0).then_inc(cleared, 1)
            pool.memset(items[:, :, :, :, 0:1], 1.0).then_inc(items_one, 1)
            pool.memset(z_q[:, JX, :], 0.0).then_inc(cleared, 1)
            pool.wait_ge(cleared, 4)
            pool.memset(z_q[ROW_ONE:ROW_ONE + 1, JX, :], 1.0).then_inc(zx_clear, 1)
            pool.wait_ge(zx_clear, 1)
            pool.wait_ge(ids_in, 16)

            def span(c):
                return 2 * chunk_pairs(c)[0], 2 * len(chunk_pairs(c))

            def indices(k, c):
                lo, n = span(c)
                wait(pool, gathered[c], 16 * n * k)
                pool.tensor_tensor(index[:, lo:lo + n], ids[:, bass.ds(k * 2 * PAIRS + lo, n)],
                                   base[:, lo:lo + n], ALU.add).then_inc(index_ready, 1)

            def gathers(k, c):
                lo, n = span(c)
                wait(pool, u_done, CHUNKS * (k - 1) + c + 1)
                pool.wait_ge(index_ready, CHUNKS * k + c + 1)
                indices(*((k, c + 1) if c + 1 < CHUNKS else (k + 1, 0)))
                for t in range(lo, lo + n):
                    pool.indirect_dma_start(
                        e[:, t, :], None, a["table"],
                        bass.IndirectOffsetOnAxis(ap=index[:, t:t + 1], axis=0),
                    ).then_inc(gathered[c], 16)

            def tile(k):
                for c in range(CHUNKS):
                    gathers(k, c)

            indices(0, 0)
            tile(0)
            with pool.Fori(1, TILES) as k:
                tile(k)

        @block.tensor
        def _(pe):
            def transposes(k, c):
                wait(pe, gathered[c], 16 * 2 * len(chunk_pairs(c)) * (k + 1))
                wait(pe, et_copied, CHUNKS * k + c)
                for n, s in enumerate(chunk_pairs(c)):
                    last = pe.transpose(p_tr[:, n * P:(n + 1) * P],
                                        e[:, 2 * s:2 * s + 2, :].rearrange("p h d -> p (h d)"),
                                        ident[:, :])
                last.then_inc(tr_done, 1)

            def e_gram(k, c):
                q = CHUNKS * k + c
                wait(pe, et_copied, q + 1)
                wait(pe, prod_done, q)
                for n, s in enumerate(chunk_pairs(c)):
                    last = pe.matmul(p_eg[:, n * P:(n + 1) * P], e_t[:, c % 2, n * P:(n + 1) * P],
                                     gram_w[:, :], start=True, stop=True)
                last.then_inc(eg_done, 1)

            def fields(k, c):
                q = CHUNKS * k + c
                wait(pe, e_scaled, q + 1)
                wait(pe, u_split, q - 1)
                for s in chunk_pairs(c):
                    lo, hi = touched(s)
                    for bk in range(lo // CB, hi // CB + 1):
                        b0, b1_ = max(lo, bk * CB), min(hi, bk * CB + CB - 1)
                        if bk > c:
                            wait(pe, u_split, q)
                        for h in range(2):
                            last = pe.matmul(
                                p_u[bk % 2][HALF * h:HALF * h + HALF,
                                            (b0 - bk * CB) * PROJ:(b1_ + 1 - bk * CB) * PROJ],
                                e[:, 2 * s + h, :],
                                wt[:, s, b0 - lo:b1_ + 1 - lo, :].rearrange("p b j -> p (b j)"),
                                start=b0 == bk * CB and P * s <= bk * CB * FIELDS,
                                stop=b1_ == bk * CB + CB - 1, skip_group_check=True)
                last.then_inc(u_done, 1)

            def project(k, c):
                q = CHUNKS * k + c
                for h in range(2):
                    wait(pe, y_normed, 2 * (q - 1) + h + 1)
                    pe.matmul(p_y[h][:, :], bias_l[:, :],
                              bias_r[:, :, :].rearrange("p b j -> p (b j)"), start=True, stop=False)
                    if h == 0:
                        wait(pe, u_high, q + 1)
                    pe.matmul(p_y[h][:, :], wg_hi[:, h, :], u_hi[:, c % 2, :], start=False, stop=False)
                    pe.matmul(p_y[h][:, :], wg_lo[:, h, :], u_hi[:, c % 2, :], start=False, stop=False)
                    if h == 0:
                        wait(pe, u_split, q + 1)
                    pe.matmul(p_y[h][:, :], wg_hi[:, h, :], u_lo[:, c % 2, :], start=False,
                              stop=True).then_inc(y_done, 1)

            def sample_gram(k, c):
                q = CHUNKS * k + c
                wait(pe, y_normed, 2 * q + 2)
                wait(pe, x_placed, q + 1)
                wait(pe, gr_copied, q)
                for h in range(2):
                    for g in range(CG):
                        at = (h * CG + g) * ITEM
                        for b in range(4):
                            it = items[:, c, h, 4 * g + b, :]
                            last = pe.matmul(p_gr[PROJ * b:PROJ * b + PROJ, at:at + ITEM],
                                             it[:, 2:ITEM], it[:, :], start=True, stop=True)
                last.then_inc(gr_done, 1)

            def interact(k):
                pe.wait_ge(we_ready, 1)
                wait(pe, h2_ready, k)
                for n, js in enumerate(Z_PARTS):
                    wait(pe, z_high, 2 * k + n + 1)
                    for j in js:
                        pe.matmul(p_o[:, :], z_hi[:, j, :], we_hi[:, j, :], start=(j == 0), stop=False)
                        pe.matmul(p_o[:, :], z_hi[:, j, :], we_lo[:, j, :], start=False, stop=False)
                    wait(pe, z_split, 2 * k + n + 1)
                    for j in js:
                        last = pe.matmul(p_o[:, :], z_lo[:, j, :], we_hi[:, j, :], start=False,
                                         stop=(j == KX - 1))
                last.then_inc(fin_done, 1)

            def turn_z(k):
                wait(pe, z_ready, k + 1)
                for n in range(KEPT // P):
                    last = pe.transpose(p_o[:, n * P:(n + 1) * P], z[:, n * P:(n + 1) * P], ident[:, :])
                last.then_inc(zt_done, 1)

            def hidden1(k):
                wait(pe, h0_ready, k + 1)
                for m in range(HID1 // P):
                    for n in range(KEPT // P):
                        last = pe.matmul(p_o[:, m * P:(m + 1) * P], w1[:, n, m * P:(m + 1) * P],
                                         h0[:, n, :], start=(n == 0), stop=(n == KEPT // P - 1))
                last.then_inc(h1_done, 1)

            def hidden2(k):
                wait(pe, h1_ready, k + 1)
                for m in range(HID2 // P):
                    for n in range(HID1 // P):
                        last = pe.matmul(p_o[:, m * P:(m + 1) * P], w2[:, n, m * P:(m + 1) * P],
                                         h1[:, n, :], start=(n == 0), stop=(n == HID1 // P - 1))
                last.then_inc(h2_done, 1)

            def result(bank, samples):
                for n in range(HID2 // P):
                    last = pe.matmul(bank[0:1, samples], w3[:, n:n + 1], h2[:, n, samples],
                                     start=(n == 0), stop=(n == HID2 // P - 1))
                last.then_inc(y_done_pe, 1)

            def x_product():
                pe.wait_ge(x_in, 16)
                for t in range(TILES):
                    for n in range(2):
                        last = pe.matmul(p_o[:, t * EMB:(t + 1) * EMB],
                                         dense_t[:, n, t * P:(t + 1) * P], wd[:, n, :],
                                         start=(n == 0), stop=(n == 1))
                last.then_inc(pe_x, 1)

            def x_turn():
                pe.wait_ge(xn_ready, 1)
                for t in range(TILES):
                    last = pe.transpose(p_o[:, t * P:(t + 1) * P], xn[:, t, :], ident[:, :])
                last.then_inc(pe_xt, 1)

            def x_sum():
                pe.wait_ge(xt_ready, 1)
                pe.wait_ge(ones_ready, 1)
                pe.matmul(p_o[ROW_SUMX:ROW_SUMX + 1, :], ones[:, :], x_t[:, :], start=True,
                          stop=True).then_inc(pe_sumx, 1)

            def dense_hidden(m):
                pe.wait_ge(w1_in, 32)
                if m == DENSE_BANKS:
                    pe.wait_ge(d1_ready, 1)
                for n in range(DENSE // P):
                    last = pe.matmul(p_d[m % DENSE_BANKS][:, :], w1_dense[:, n, m * P:(m + 1) * P],
                                     dense_t[:, n, :], start=(n == 0), stop=(n == DENSE // P - 1))
                last.then_inc(pe_d1, 1)

            def extra_weights():
                pe.wait_ge(mix_ready, 1)
                pe.wait_ge(wl_in, 48)
                pe.wait_ge(sumx_ready, 1)
                for j in range(KX):
                    last = pe.matmul(p_o[:, :], mix[:, j, :], wl[:, j, :], start=(j == 0),
                                     stop=(j == KX - 1))
                last.then_inc(pe_wx, 1)

            pe.wait_ge(ws_in, 16)
            pe.matmul(p_o[:, 0:P], center[:, :], ws[:, :].unsqueeze(1).to_broadcast([EMB, 2, DIM]),
                      start=True, stop=True).then_inc(pe_wc, 1)
            pe.wait_ge(wc_ready, 1)
            pe.matmul(p_gr[:, 0:P], wc[:, :, :].rearrange("p h d -> p (h d)"),
                      wc[:, :, :].rearrange("p h d -> p (h d)"), start=True, stop=True).then_inc(pe_gram, 1)
            pe.wait_ge(wg_ready, 1)
            pe.transpose(p_o[:, 0:P], wg[:, :, :].rearrange("p h d -> p (h d)"),
                         ident[:, :]).then_inc(pe_wg, 1)
            pe.wait_ge(half_ready, 1)
            x_product()

            dense_hidden(0)
            dense_hidden(1)
            for c in range(CHUNKS):
                transposes(0, c)
                if c == 0:
                    dense_hidden(2)
                e_gram(0, c)
                if c == 0:
                    x_turn()
                    dense_hidden(3)
                    pe.wait_ge(wt_ready, 1)
                else:
                    if c == 1:
                        pe.wait_ge(bias_ready, 1)
                        pe.wait_ge(d1_ready, HID1 // P)
                        x_sum()
                    project(0, c - 1)
                    if c >= 2:
                        pe.wait_ge(items_one, 1)
                        sample_gram(0, c - 2)
                    if c == CHUNKS - 1:
                        extra_weights()
                fields(0, c)

            pe.wait_ge(mlp_in, 32)
            with pe.Fori(1, TILES) as k:
                for c in range(CHUNKS):
                    transposes(k, c)
                    if c == 3:
                        turn_z(k - 1)
                    e_gram(k, c)
                    project(*before(k, c, 1))
                    sample_gram(*before(k, c, 2))
                    if c == 2:
                        interact(k - 1)
                    if c == 3:
                        hidden1(k - 1)
                    fields(k, c)
                    if c == 3:
                        hidden2(k - 1)
            k = TILES - 1
            sample_gram(k, CHUNKS - 2)
            project(k, CHUNKS - 1)
            pe.wait_ge(h2_ready, k)
            result(p_o, slice(0, k * P))
            sample_gram(k, CHUNKS - 1)
            pe.wait_ge(y_ready, 1)
            interact(k)
            turn_z(k)
            hidden1(k)
            hidden2(k)
            pe.wait_ge(h2_ready, k + 1)
            result(p_o, slice(k * P, BATCH))

        @block.vector
        def _(dve):
            count = [0]

            def link(ins):
                count[0] += 1
                ins.then_inc(dve_setup, 1)
                dve.wait_ge(dve_setup, count[0])

            def bcast(ap, n):
                return ap.unsqueeze(2).to_broadcast([ap.shape[0], ap.shape[1], n])

            dve.memset(eps[:, :], EPS).then_inc(eps_ready, 1)
            dve.memset(ones[:, :], 1.0).then_inc(ones_ready, 1)
            link(dve.memset(gram_w[:, :], 0.0))
            link(dve.memset(wg_hi[:, :, :].bitcast(F32), 0.0))
            link(dve.memset(wg_lo[:, :, :].bitcast(F32), 0.0))
            dve.wait_ge(pe_wc, 1)
            dve.tensor_copy(wc[:, :, :].rearrange("p h d -> p (h d)"), p_o[:, 0:P]).then_inc(wc_ready, 1)
            dve.tensor_scalar(wg[:, :, :].rearrange("p h d -> p (h d)"), p_o[:, 0:P], gs[:, 0:1], None,
                              ALU.mult).then_inc(wg_ready, 1)
            dve.wait_ge(pe_gram, 1)
            for h in range(2):
                r = slice(DIM * h, DIM * h + DIM)
                last = dve.tensor_copy(gram_w[r, r], p_gr[r, r])
            last.then_inc(gram_ready, 1)
            dve.wait_ge(pe_wg, 1)
            for h in range(2):
                r = slice(DIM * h, DIM * h + DIM)
                link(dve.tensor_copy(wg_hi[r, h, :], p_o[r, 0:P]))
                last = dve.tensor_tensor(wg_lo[r, h, :], p_o[r, 0:P], wg_hi[r, h, :].bitcast(F32),
                                         ALU.subtract)
            last.then_inc(half_ready, 1)
            dve.wait_ge(wsi_in, 16)
            link(dve.tensor_reduce(wsi_mean[:, :], wsi[:, :, :], AX_X, ALU.add))
            link(dve.tensor_scalar(wsi_mean[:, :], wsi_mean[:, :], 1.0 / PROJ, None, ALU.mult))
            link(dve.tensor_tensor(wsi[:, :, :], wsi[:, :, :], bcast(wsi_mean[:, :], PROJ), ALU.subtract))
            dve.tensor_tensor(
                wt[:, :, :, :], wsi[:, :, :].unsqueeze(2).to_broadcast([P, PAIRS, TOUCH, PROJ]),
                touch[:, :, :].unsqueeze(3).to_broadcast([P, PAIRS, TOUCH, PROJ]),
                ALU.mult).then_inc(wt_ready, 1)

            def x_norm():
                dve.wait_ge(pe_x, 1)
                for t in range(TILES):
                    last = dve.bn_stats(x_stats[:, t, :], p_o[:, t * EMB:(t + 1) * EMB])
                link(last)
                for t in range(TILES):
                    last = dve.bn_aggr(x_mv[:, t, :], x_stats[:, t, :])
                last.then_inc(x_agg, 1)
                dve.wait_ge(x_root, 1)
                link(dve.reciprocal(x_rs[:, :], x_sd[:, :]))
                for t in range(TILES):
                    last = dve.tensor_scalar(xn[:, t, :], p_o[:, t * EMB:(t + 1) * EMB],
                                             x_mv[:, t, 0:1], x_rs[:, t:t + 1], ALU.subtract, ALU.mult)
                last.then_inc(xn_ready, 1)

            def bias():
                dve.wait_ge(bias_in, 16)
                dve.wait_ge(cleared, 4)
                link(dve.tensor_reduce(wsum4[:, :], wsi4[:, :, :], AX_X, ALU.add))
                link(dve.tensor_reduce(wmean4[:, :], wsum4[:, :], AX_X, ALU.add))
                link(dve.tensor_scalar(wmean4[:, :], wmean4[:, :], 1.0 / PROJ, None, ALU.mult))
                link(dve.tensor_scalar(wsum4[:, :], wsum4[:, :], wmean4[:, 0:1], None, ALU.subtract))

                def parts(value, n, masks, dst):
                    hi = split_h[:, 0:n]
                    link(dve.tensor_copy(hi, value))
                    link(dve.tensor_tensor(split_r[:, 0:n], value, hi.bitcast(F32), ALU.subtract))
                    link(dve.tensor_scalar(split_t[:, 0:n], hi.bitcast(F32), part4[:, masks:masks + 1],
                                           None, ALU.mult))
                    link(dve.scalar_tensor_tensor(dst, split_r[:, 0:n], part4[:, masks + 1:masks + 2],
                                                  split_t[:, 0:n], ALU.mult, ALU.add))

                parts(bs4[:, :], EMB, 0, bias_l[0:PARTS ** 2, :])
                parts(wsum4[:, :], PROJ, PARTS, bias_w[:, :])
                dve.tensor_copy(bias_r[0:PARTS ** 2, :, :], bias_w[:, :].unsqueeze(1).to_broadcast(
                    [PARTS ** 2, CB, PROJ])).then_inc(bias_ready, 1)

            def mixing():
                dve.wait_ge(wl_in, 48)
                dve.wait_ge(cleared, 4)
                dve.tensor_scalar(scale_w[:, :], g_c, g_i, None, ALU.mult).then_inc(scale_ready, 1)
                dve.tensor_scalar(mix[:, 0:JX, 0:PROJ], is_col, b_i, None, ALU.mult)
                link(dve.tensor_tensor(mix_t[:, :, :], is_row.unsqueeze(1).to_broadcast([P, JX, PROJ]),
                                       bcast(b_c, PROJ), ALU.mult))
                link(dve.tensor_tensor(mix[:, 0:JX, 0:PROJ], mix[:, 0:JX, 0:PROJ], mix_t[:, :, :], ALU.add))
                dve.tensor_scalar(mix[:, 0:JX, ROW_ONE], b_c, b_i, float(EMB), ALU.mult, ALU.mult)
                mine = slice(ROW_X, ROW_X + PROJ)
                dve.tensor_copy(mix[mine, JX, mine], is_row[mine, :])
                dve.tensor_copy(mix[mine, JX, ROW_SUMX:ROW_SUMX + 1], b_i[mine, :]).then_inc(mix_ready, 1)

            def weights_low(js):
                dve.wait_ge(scale_ready, 1)
                for j in js:
                    dve.wait_ge(we_hi_ready, j + 1)
                    dve.scalar_tensor_tensor(we_lo[:, j, :], wl[:, j, :], scale_w[:, j:j + 1],
                                             we_hi[:, j, :].bitcast(F32), ALU.mult, ALU.subtract)

            def rows(k, c):
                q = CHUNKS * k + c
                pairs = chunk_pairs(c)
                n, at = 2 * len(pairs), 2 * pairs[0]
                dve.wait_ge(eg_done, q + 1)
                mine = e[:, at:at + n, :]
                dve.tensor_tensor(prod[:, 0:n * DIM], mine.rearrange("p t d -> p (t d)"),
                                  p_eg[:, 0:n * DIM], ALU.mult).then_inc(prod_done, 1)
                dve.wait_ge(prod_done, q + 1)
                dve.tensor_reduce(ss[:, 0:n], prod[:, 0:n * DIM].rearrange("p (t d) -> p t d", d=DIM),
                                  AX_X, ALU.add).then_inc(ss_done, 1)
                dve.wait_ge(ss_done, q + 1)
                dve.tensor_scalar(var[:, 0:n], ss[:, 0:n], 1.0 / EMB, 0.0, ALU.mult,
                                  ALU.max).then_inc(var_done, 1)
                dve.wait_ge(sd_done, q + 1)
                dve.reciprocal(rs[:, 0:n], sd[:, 0:n]).then_inc(rs_done, 1)
                dve.wait_ge(rs_done, q + 1)
                dve.tensor_tensor(mine, mine, bcast(rs[:, 0:n], DIM), ALU.mult).then_inc(e_scaled, 1)

            def norm(k, c):
                q = CHUNKS * k + c
                for h in range(2):
                    dve.wait_ge(sq_done, 2 * q + h + 1)
                    dve.tensor_reduce(ss2[:, h, :], sq[:, h, :].rearrange("p (b j) -> p b j", j=PROJ),
                                      AX_X, ALU.add).then_inc(ss2_done, 1)
                for h in range(2):
                    dve.wait_ge(sd2_done, 2 * q + h + 1)
                    dve.reciprocal(rs2[:, h, :], sd2[:, h, :]).then_inc(rs2_done, 1)
                wait(dve, gr_done, q - CHUNKS + 1)
                for h in range(2):
                    dve.wait_ge(rs2_done, 2 * q + h + 1)
                    dve.tensor_tensor(items[:, c, h, :, 2:ITEM],
                                      p_y[h][:, :].rearrange("p (b j) -> p b j", j=PROJ),
                                      bcast(rs2[:, h, :], PROJ), ALU.mult).then_inc(y_normed, 1)

            def low_u(k, c):
                q = CHUNKS * k + c
                dve.wait_ge(u_high, q + 1)
                dve.tensor_tensor(u_lo[:, c % 2, :], p_u[c % 2][:, :], u_hi[:, c % 2, :].bitcast(F32),
                                  ALU.subtract).then_inc(u_split, 1)

            def move(k):
                dve.wait_ge(gr_copied, CHUNKS * k + CHUNKS)
                wait(dve, z_high, 2 * k)
                for b in range(4):
                    dve.tensor_copy(z_q[0:PROJ, JX, b::4], z_s[PROJ * b:PROJ * b + PROJ, :, 0])
                dve.copy_predicated(z_s[:, :, 2:2 + BLOCKS],
                                    second[:, :].unsqueeze(1).to_broadcast([P, GROUPS, BLOCKS]),
                                    z_s[:, :, 2 + BLOCKS:ITEM]).then_inc(merged, 1)
                dve.wait_ge(merged, k + 1)
                for b in range(4):
                    for jj in range(3):
                        last = move_columns(dve.tensor_copy, b, jj)
                last.then_inc(moved_dve, 1)

            def low_z(k):
                for n, js in enumerate(Z_PARTS):
                    dve.wait_ge(z_high, 2 * k + n + 1)
                    if n == 0:
                        wait(dve, fin_done, k)
                    js = slice(js[0], js[-1] + 1)
                    dve.tensor_tensor(z_lo[:, js, :], z_q[:, js, :], z_hi[:, js, :].bitcast(F32),
                                      ALU.subtract).then_inc(z_split, 1)

            def out_norm(k):
                dve.wait_ge(fin_done, k + 1)
                dve.bn_stats(o_stats[:, :], p_o[:, :])
                dve.drain()
                dve.bn_aggr(o_mv[:, :], o_stats[:, :]).then_inc(o_agg, 1)
                dve.wait_ge(o_root, k + 1)
                dve.reciprocal(o_rs[:, :], o_sd[:, :]).then_inc(o_recip, 1)
                dve.wait_ge(o_recip, k + 1)
                dve.tensor_scalar(z[:, :], p_o[:, 0:KEPT], o_mv[:, 0:1], o_rs[:, 0:1], ALU.subtract,
                                  ALU.mult).then_inc(z_ready, 1)

            def add_dense(k):
                dve.wait_ge(h1_done, k + 1)
                dve.tensor_tensor(h1_sum[:, :, :], p_o[:, :].rearrange("p (m b) -> p m b", b=P),
                                  d1[:, :, bass.ds(k * P, P)], ALU.add).then_inc(h1_added, 1)

            for c in range(CHUNKS):
                if c == 0:
                    x_norm()
                rows(0, c)
                if c == 0:
                    bias()
                else:
                    norm(0, c - 1)
                if c == 2:
                    mixing()
                low_u(0, c)
            weights_low(range(JX))
            dve.wait_ge(wx_hi_ready, 1)
            dve.scalar_tensor_tensor(we_lo[:, JX, :], p_o[:, :], row_scale[:, 0:1],
                                     we_hi[:, JX, :].bitcast(F32), ALU.mult,
                                     ALU.subtract).then_inc(we_ready, 1)
            with dve.Fori(1, TILES) as k:
                for c in range(CHUNKS):
                    if c == 2:
                        low_z(k - 1)
                    rows(k, c)
                    norm(*before(k, c, 1))
                    if c == 1:
                        move(k - 1)
                    if c == 2:
                        out_norm(k - 1)
                    if c == 3:
                        add_dense(k - 1)
                    low_u(k, c)
            k = TILES - 1
            norm(k, CHUNKS - 1)
            move(k)
            low_z(k)
            out_norm(k)
            add_dense(k)

        @block.scalar
        def _(act):
            for signal, dst, name in ((ws_in, setup[:, :], "setup"), (wsi_in, wsi_touch[:, :, :], "wsi_touch"),
                                      (bias_in, bias4[:, :], "bias4")):
                act.dma_start(dst, a[name]).then_inc(signal, 16)

            def root(dst, src, scale):
                return act.activation(dst, src, ACT.Sqrt, bias=eps[0:dst.shape[0], 0:1], scale=scale)

            def copy_et(k, c):
                q = CHUNKS * k + c
                n = len(chunk_pairs(c)) * P
                act.wait_ge(tr_done, q + 1)
                wait(act, eg_done, q - 1)
                act.activation(e_t[:, c % 2, 0:n], p_tr[:, 0:n], ACT.Copy).then_inc(et_copied, 1)

            def row_root(k, c):
                q = CHUNKS * k + c
                n = 2 * len(chunk_pairs(c))
                act.wait_ge(var_done, q + 1)
                wait(act, rs_done, q)
                root(sd[:, 0:n], var[:, 0:n], 1.0).then_inc(sd_done, 1)

            def squares(k, c):
                q = CHUNKS * k + c
                for h in range(2):
                    act.wait_ge(y_done, 2 * q + h + 1)
                    wait(act, ss2_done, 2 * (q - 1) + h + 1)
                    act.activation(sq[:, h, :], p_y[h][:, :], ACT.Square).then_inc(sq_done, 1)
                for h in range(2):
                    act.wait_ge(ss2_done, 2 * q + h + 1)
                    wait(act, rs2_done, 2 * (q - 1) + h + 1)
                    root(sd2[:, h, :], ss2[:, h, :], 1.0 / PROJ).then_inc(sd2_done, 1)

            def place_x(k, c):
                q = CHUNKS * k + c
                wait(act, gr_done, q - CHUNKS + 1)
                act.activation(items[:, c, :, :, 1],
                               x_t[:, bass.ds(k * P, P)].rearrange("p (h b) -> p h b", h=2)
                               [:, :, CB * c:CB * c + CB], ACT.Copy).then_inc(x_placed, 1)

            def high_u(k, c):
                q = CHUNKS * k + c
                act.wait_ge(u_done, q + 1)
                wait(act, y_done, 2 * (q - 1))
                act.activation(u_hi[:, c % 2, :], p_u[c % 2][:, :], ACT.Copy).then_inc(u_high, 1)

            def copy_gram(k, c):
                act.wait_ge(gr_done, CHUNKS * k + c + 1)
                wait(act, moved_dve, k)
                wait(act, moved_act, k)
                per_half = GROUPS // 2
                for h in range(2):
                    at = per_half * h + CG * c
                    last = act.activation(
                        z_s[:, at:at + CG, :],
                        p_gr[:, h * CG * ITEM:(h + 1) * CG * ITEM]
                        .rearrange("p (g j) -> p g j", j=ITEM), ACT.Copy)
                last.then_inc(gr_copied, 1)

            def move(k):
                act.wait_ge(gr_copied, CHUNKS * k + CHUNKS)
                wait(act, z_split, 2 * k)
                act.activation(z_q[ROW_SUMX:ROW_SUMX + 1, JX, :],
                               sumx[ROW_SUMX:ROW_SUMX + 1, bass.ds(k * P, P)], ACT.Copy)
                for b in range(4):
                    act.copy(z_q[ROW_X:ROW_X + PROJ, JX, b::4], z_s[PROJ * b:PROJ * b + PROJ, :, 1])
                act.wait_ge(merged, k + 1)
                for b in range(4):
                    last = move_columns(act.copy, b, 3)
                last.then_inc(moved_act, 1)

            def high_z(k):
                act.wait_ge(moved_act, k + 1)
                act.wait_ge(moved_dve, k + 1)
                wait(act, fin_done, k)
                for js in Z_PARTS:
                    js = slice(js[0], js[-1] + 1)
                    act.activation(z_hi[:, js, :], z_q[:, js, :], ACT.Copy).then_inc(z_high, 1)

            def dense_bias(m):
                act.wait_ge(pe_d1, m + 1)
                act.wait_ge(w1_in, 32)
                act.activation(d1[:, m, :], p_d[m % DENSE_BANKS][:, :], ACT.Identity,
                               bias=b1[:, m:m + 1]).then_inc(d1_ready, 1)

            def out_root(k):
                act.wait_ge(o_agg, k + 1)
                root(o_sd[:, :], o_mv[:, 1:2], 1.0).then_inc(o_root, 1)

            def gain_z(k):
                act.wait_ge(zt_done, k + 1)
                wait(act, h1_done, k)
                for n in range(KEPT // P):
                    last = act.activation(h0[:, n, :], p_o[:, n * P:(n + 1) * P], ACT.Identity,
                                          bias=glb[:, 1, n:n + 1], scale=glb[:, 0, n:n + 1])
                last.then_inc(h0_ready, 1)

            def relu1(k):
                act.wait_ge(h1_added, k + 1)
                wait(act, h2_done, k)
                act.activation(h1[:, :, :], h1_sum[:, :, :], ACT.Relu).then_inc(h1_ready, 1)

            def relu2(k):
                act.wait_ge(h2_done, k + 1)
                for n in range(HID2 // P):
                    last = act.activation(h2[:, n, bass.ds(k * P, P)], p_o[:, n * P:(n + 1) * P],
                                          ACT.Relu, bias=b2[:, n:n + 1])
                last.then_inc(h2_ready, 1)

            def copy_y(samples, n):
                act.wait_ge(y_done_pe, n)
                act.activation(y_row[:, samples], p_o[0:1, samples], ACT.Copy).then_inc(y_ready, 1)

            act.wait_ge(eps_ready, 1)
            root(warm[:, :], eps[:, :], 1.0)
            act.wait_ge(x_agg, 1)
            root(x_sd[:, :], x_mv[:, :, 1], 1.0).then_inc(x_root, 1)
            dense_bias(0)
            for c in range(CHUNKS):
                copy_et(0, c)
                if c == 0:
                    dense_bias(1)
                    dense_bias(2)
                row_root(0, c)
                if c == 0:
                    act.wait_ge(pe_xt, 1)
                    act.activation(x_t[:, :], p_o[:, :], ACT.Identity, bias=gdb[:, 1:2],
                                   scale=gdb[:, 0:1]).then_inc(xt_ready, 1)
                    act.wait_ge(xt_ready, 1)
                    dense_bias(3)
                else:
                    if c == 1:
                        act.wait_ge(pe_sumx, 1)
                        act.activation(sumx[ROW_SUMX:ROW_SUMX + 1, :], p_o[ROW_SUMX:ROW_SUMX + 1, :],
                                       ACT.Copy).then_inc(sumx_ready, 1)
                    squares(0, c - 1)
                    if c >= 2:
                        copy_gram(0, c - 2)
                place_x(0, c)
                high_u(0, c)
                if c >= 2:
                    act.wait_ge(scale_ready, 1)
                    half = JX // 2
                    for j in range(half * (c - 2), half * (c - 1)):
                        act.activation(we_hi[:, j, :], wl[:, j, :], ACT.Copy,
                                       scale=scale_w[:, j:j + 1]).then_inc(we_hi_ready, 1)
            act.wait_ge(pe_wx, 1)
            act.activation(we_hi[:, JX, :], p_o[:, :], ACT.Copy,
                           scale=row_scale[:, 0:1]).then_inc(wx_hi_ready, 1)
            act.wait_ge(zx_clear, 1)
            act.wait_ge(mlp_in, 32)
            act.wait_ge(sumx_ready, 1)
            with act.Fori(1, TILES) as k:
                for c in range(CHUNKS):
                    copy_et(k, c)
                    if c == 3:
                        gain_z(k - 1)
                    if c == 2:
                        high_z(k - 1)
                    row_root(k, c)
                    squares(*before(k, c, 1))
                    copy_gram(*before(k, c, 2))
                    place_x(k, c)
                    if c == 1:
                        move(k - 1)
                    if c == 2:
                        out_root(k - 1)
                    if c == 3:
                        relu1(k - 1)
                    high_u(k, c)
                    if c == 3:
                        relu2(k - 1)
            k = TILES - 1
            copy_gram(k, CHUNKS - 2)
            squares(k, CHUNKS - 1)
            copy_y(slice(0, k * P), 1)
            copy_gram(k, CHUNKS - 1)
            move(k)
            high_z(k)
            out_root(k)
            gain_z(k)
            relu1(k)
            relu2(k)
            copy_y(slice(k * P, BATCH), 2)


def before(k, c, n):
    return (k, c - n) if c >= n else (k - 1, c - n + CHUNKS)


def kernel(**inputs):
    import numpy as np
    import concourse.bacc as bacc
    from concourse.bass_utils import run_bass_kernel_spmd

    def arr(name):
        return np.asarray(inputs[name])

    tables = [arr(f"tbl_{f}") for f in range(FIELDS)]
    starts = np.concatenate([[0], np.cumsum([t.shape[0] for t in tables])[:-1]]).astype(np.int32)
    rows = np.arange(PAIRS * P).reshape(PAIRS, P)
    field, sample = rows % FIELDS, rows // FIELDS
    part = np.arange(P)
    row_i, quad = part % PROJ, part // PROJ
    past = (row_i[:, None] - JX * quad[:, None] - np.arange(JX)) % PROJ
    col = JX * quad[:, None] + np.arange(JX) + BLOCKS * ((past == 0) | (past > BLOCKS))
    high, low = np.maximum(row_i[:, None], col) + 1, np.minimum(row_i[:, None], col) + 1
    wl_t = arr("L0_rec_Wl").T
    wl_pairs = np.where((past > 0)[:, :, None], wl_t[np.where(past > 0, high * (high - 1) // 2 + low, 0)],
                        np.float32(0))
    has_x = (part >= ROW_X) & (part < ROW_X + PROJ)
    wl_x = np.where(has_x[:, None], wl_t[(row_i + 1) * row_i // 2], np.float32(0))
    past_block = (row_i[:, None] - np.arange(BLOCKS)) % PROJ
    gsi, bsi = arr("L0_rec_gsi"), arr("L0_rec_bsi")
    wsi_a = arr("L0_rec_Wsi")
    r4 = np.arange(PARTS ** 2)
    pick = np.concatenate([r4[:, None] // PARTS == np.arange(PARTS), r4[:, None] % PARTS == np.arange(PARTS)], 1)
    f32 = np.float32

    def split_rows(w, n):
        return w.reshape(n, P, -1).transpose(1, 0, 2)

    def beside(*parts):
        return np.concatenate([p.reshape(p.shape[0], -1) for p in parts], 1)

    ids = arr("ids").reshape(TILES, 2, PAIRS, P).transpose(3, 0, 2, 1).reshape(P, -1)
    touch = (sample.T[:, :, None] - (P * np.arange(PAIRS) // FIELDS)[None, :, None] == np.arange(TOUCH))
    arrays = {
        "table": np.concatenate(tables, 0),
        "rows_in": beside(np.repeat(starts[field.T], 2, 1), ids, np.zeros_like(ids[:, :2 * PAIRS])),
        "setup": beside(np.eye(P, dtype=f32), (np.eye(P) - 1.0 / P).astype(f32), arr("L0_rec_Ws"),
                        arr("L0_rec_gs")[:, None]),
        "wsi_touch": np.concatenate([wsi_a.T[field].transpose(1, 0, 2), touch.astype(f32)], 2),
        "dense_wd": np.concatenate([split_rows(arr("r_dense_t").T, 2), split_rows(arr("L0_rec_Wd").T, 2),
                                    np.stack([arr("L0_rec_gd"), arr("L0_rec_bd")], 1)[:, :, None]], 2),
        "bias4": np.concatenate([
            np.tile(wsi_a.reshape(1, -1), (PARTS ** 2, 1)),
            np.tile(arr("L0_rec_bs")[None], (PARTS ** 2, 1)), pick.astype(f32)], 1),
        "wl": np.concatenate([wl_pairs, wl_x[:, None]], 1),
        "fold": beside(
            gsi[row_i][:, None], bsi[row_i][:, None],
            np.where(has_x | (part < PROJ), gsi[row_i], f32(1))[:, None], gsi[col], bsi[col],
            (row_i[:, None] == np.arange(PROJ)).astype(f32),
            (col[:, :, None] == np.arange(PROJ)).astype(f32)),
        "second": ((past_block == 0) | (past_block > BLOCKS)).astype(np.int32),
        "biases": beside(arr("b_top1").reshape(-1, P).T, arr("b_top2").reshape(-1, P).T,
                         arr("L0_rec_gl")[:KEPT].reshape(-1, P).T, arr("L0_rec_bl")[:KEPT].reshape(-1, P).T),
        "w1": split_rows(arr("W_top1")[:KEPT], KEPT // P),
        "w1_dense": split_rows(arr("W_top1")[MAXD:], DENSE // P),
        "w2_w3": beside(split_rows(arr("W_top2"), HID1 // P), arr("W_top3").reshape(-1, P).T),
    }
    arrays = {name: np.ascontiguousarray(x) for name, x in arrays.items()}

    nc = bacc.Bacc("TRN2", target_bir_lowering=False, num_devices=1)
    aps = {name: nc.dram_tensor(f"in_{name}", x.shape, mybir.dt.from_np(x.dtype), kind="ExternalInput").ap()
           for name, x in arrays.items()}
    out = nc.dram_tensor("out_y", (1, BATCH), F32, kind="ExternalOutput").ap()
    build(nc, aps, out)
    r = run_bass_kernel_spmd(nc, [{f"in_{name}": x for name, x in arrays.items()}], core_ids=[0])
    return r.results[0]["out_y"].reshape(BATCH, 1)
```

```python
from contextlib import ExitStack

import concourse.bass as bass
from concourse import mybir

F32 = mybir.dt.float32
F32R = mybir.dt.float32r
I32 = mybir.dt.int32
ALU = mybir.AluOpType
ACT = mybir.ActivationFunctionType
AX_X = mybir.AxisListType.X

P = 128
BATCH = 512
FIELDS = 26
DIM = 64
EMB = 128
PROJ = 32
DENSE = 256
MAXD = 512
KEPT = 384
HID1, HID2 = 512, 256
EPS = 1e-5

TILES = BATCH // P
HALF = P // 2
PAIRS = HALF * FIELDS // P
CHUNKS = 4
CB = HALF // CHUNKS
BANK = CB * PROJ
TOUCH = 6
ITEM = PROJ + 2
GROUPS = P // 4
CG = CB // 4
BLOCKS = PROJ // 2
JX = BLOCKS // 4
KX = JX + 1
DENSE_BANKS = 3
DVE_MOVES, ACT_MOVES = (0,), (1, 2, 3)
EARLY_DVE_MOVES, EARLY_ACT_MOVES = (0, 1), (2, 3)
LATE_DVE_MOVES, LATE_ACT_MOVES = (0, 1, 2), (3,)
ROW_SUMX, ROW_X, ROW_ONE = 32, 64, 96
PARTS = 2


def chunk_pairs(c):
    last = [((c1 + 1) * CB * FIELDS - 1) // P for c1 in range(CHUNKS)]
    return range(0 if c == 0 else last[c - 1] + 1, last[c] + 1)


def touched(s):
    return P * s // FIELDS, (P * s + P - 1) // FIELDS


ALL_GROUPS = (0, GROUPS // 2)
EARLY, LATE = (0, GROUPS // 2 - CG), (GROUPS // 2 - CG, GROUPS // 2)
TURN_FIRST = (1, 2)
Z_PARTS = (range(0, KX // 2), range(KX // 2, KX))
UNIT_HALVES = (range(0, HID1 // P // 2), range(HID1 // P // 2, HID1 // P))
MOST = max(len(chunk_pairs(c)) for c in range(CHUNKS))


def build(nc, a, out):
    with ExitStack() as ctx:
        def sb(name, shape, dt=F32):
            return ctx.enter_context(nc.sbuf_tensor(name, shape, dt))

        def bank(name):
            return ctx.enter_context(nc.psum_tensor(name, [P, 512], F32))

        def sem(name):
            return ctx.enter_context(nc.semaphore(name))

        rows_in = sb("rows_in", [P, (TILES + 2) * 2 * PAIRS], I32)
        base, ids = rows_in[:, 0:2 * PAIRS], rows_in[:, 2 * PAIRS:]
        index = sb("index", [P, 2 * PAIRS], I32)
        setup = sb("setup", [P, 2 * P + DIM + 1])
        ident, center = setup[:, 0:P], setup[:, P:2 * P]
        ws, gs = setup[:, 2 * P:2 * P + DIM], setup[:, 2 * P + DIM:]
        wc = sb("wc", [EMB, 2, DIM])
        wg = sb("wg", [EMB, 2, DIM])
        gram_w = sb("gram_w", [P, P])
        wg_hi = sb("wg_hi", [P, 2, EMB], F32R)
        wg_lo = sb("wg_lo", [P, 2, EMB], F32R)
        wsi_touch = sb("wsi_touch", [P, PAIRS, PROJ + TOUCH])
        wsi, touch = wsi_touch[:, :, 0:PROJ], wsi_touch[:, :, PROJ:]
        wsi_mean = sb("wsi_mean", [P, PAIRS])
        wt = sb("wt", [P, PAIRS, TOUCH, PROJ])
        bias4 = sb("bias4", [PARTS ** 2, PROJ * FIELDS + EMB + 2 * PARTS])
        wsi4 = bias4[:, 0:PROJ * FIELDS].rearrange("p (j f) -> p j f", f=FIELDS)
        bs4 = bias4[:, PROJ * FIELDS:PROJ * FIELDS + EMB]
        part4 = bias4[:, PROJ * FIELDS + EMB:]
        wsum4 = sb("wsum4", [PARTS ** 2, PROJ])
        wmean4 = sb("wmean4", [PARTS ** 2, 1])
        split_h = sb("split_h", [PARTS ** 2, EMB], F32R)
        split_r = sb("split_r", [PARTS ** 2, EMB])
        split_t = sb("split_t", [PARTS ** 2, EMB])
        bias_w = sb("bias_w", [PARTS ** 2, PROJ])
        bias_l = sb("bias_l", [P, EMB], F32R)
        bias_r = sb("bias_r", [P, CB, PROJ], F32R)
        dense_wd = sb("dense_wd", [P, 2, BATCH + EMB + 1])
        dense_t, wd = dense_wd[:, :, 0:BATCH], dense_wd[:, :, BATCH:BATCH + EMB]
        gdb = dense_wd[:, :, BATCH + EMB]
        x_stats = sb("x_stats", [P, TILES, 6])
        x_mv = sb("x_mv", [P, TILES, 2])
        x_sd = sb("x_sd", [P, TILES])
        x_rs = sb("x_rs", [P, TILES])
        xn = sb("xn", [P, TILES, EMB])
        x_t = sb("x_t", [EMB, BATCH])
        ones = sb("ones", [P, 1])
        eps = sb("eps", [P, 1])
        warm = sb("warm", [P, 1])
        sumx = sb("sumx", [P, BATCH])
        wl = sb("wl", [P, KX, MAXD])
        we_hi = sb("we_hi", [P, KX, MAXD], F32R)
        we_lo = sb("we_lo", [P, KX, MAXD], F32R)
        fold = sb("fold", [P, 3 + 2 * JX + PROJ * (1 + JX)])
        g_i, b_i, row_scale = fold[:, 0:1], fold[:, 1:2], fold[:, 2:3]
        g_c, b_c = fold[:, 3:3 + JX], fold[:, 3 + JX:3 + 2 * JX]
        is_row = fold[:, 3 + 2 * JX:3 + 2 * JX + PROJ]
        is_col = fold[:, 3 + 2 * JX + PROJ:].rearrange("p (j n) -> p j n", n=PROJ)
        second = sb("second", [P, BLOCKS], I32)
        scale_w = sb("scale_w", [P, JX])
        mix = sb("mix", [P, KX, P])
        mix_t = sb("mix_t", [P, JX, PROJ])
        biases = sb("biases", [P, HID1 // P + HID2 // P + 2 * KEPT // P])
        b1, b2 = biases[:, 0:HID1 // P], biases[:, HID1 // P:HID1 // P + HID2 // P]
        glb = biases[:, HID1 // P + HID2 // P:].rearrange("p (g n) -> p g n", g=2)
        w1 = sb("w1", [P, KEPT // P, HID1])
        w1_dense = sb("w1_dense", [P, DENSE // P, HID1])
        d1 = sb("d1", [P, HID1 // P, BATCH])
        w2_w3 = sb("w2_w3", [P, HID1 // P * HID2 + HID2 // P])
        w2 = w2_w3[:, 0:HID1 // P * HID2].rearrange("p (n m) -> p n m", m=HID2)
        w3 = w2_w3[:, HID1 // P * HID2:]

        e = sb("e", [P, 2 * PAIRS, DIM])
        e_t = sb("e_t", [P, 2, MOST * P])
        prod = sb("prod", [P, MOST * P])
        ss = sb("ss", [P, 2 * MOST])
        var = sb("var", [P, 2 * MOST])
        sd = sb("sd", [P, 2 * MOST])
        rs = sb("rs", [P, 2 * MOST])
        u_hi = sb("u_hi", [P, 2, BANK], F32R)
        u_lo = sb("u_lo", [P, 2, BANK], F32R)
        sq = sb("sq", [P, 2, BANK])
        ss2 = sb("ss2", [P, 2, CB])
        sd2 = sb("sd2", [P, 2, CB])
        rs2 = sb("rs2", [P, 2, CB])
        items = sb("items", [EMB, CHUNKS, 2, CB, ITEM])
        z_s = sb("z_s", [P, GROUPS, ITEM])
        z_q = sb("z_q", [P, KX, P])
        z_hi = sb("z_hi", [P, KX, P], F32R)
        z_lo = sb("z_lo", [P, KX, P], F32R)
        o_stats = sb("o_stats", [P, 6])
        o_mv = sb("o_mv", [P, 2])
        o_sd = sb("o_sd", [P, 1])
        o_rs = sb("o_rs", [P, 1])
        z = sb("z", [P, KEPT])
        h0 = sb("h0", [P, KEPT // P, P])
        h1_sum = sb("h1_sum", [P, HID1 // P, P])
        h1 = sb("h1", [P, HID1 // P, P])
        h2 = sb("h2", [P, HID2 // P, BATCH])
        y_row = sb("y_row", [1, BATCH])

        p_tr, p_eg, p_gr, p_o = bank("p_tr"), bank("p_eg"), bank("p_gr"), bank("p_o")
        p_u = [bank("p_u0"), bank("p_u1")]
        p_y = ctx.enter_context(nc.psum_tensor("p_y", [P, 2, 512], F32))
        last_tr, last_h = p_tr, p_eg
        last_z = p_y[:, 0, :]
        last_y = p_u[0]
        last_h1 = [p_gr[:, :], p_y[:, 1, :]]
        p_d = [p_y[:, 0, :], p_y[:, 1, :], p_gr[:, :]]

        ids_in, ws_in, wsi_in, x_in, w1_in, bias_in, wl_in, mlp_in = (
            sem(n) for n in ("ids_in", "ws_in", "wsi_in", "x_in", "w1_in", "bias_in", "wl_in", "mlp_in"))
        gathered = [sem(f"gathered{c}") for c in range(CHUNKS)]
        index_ready, dve_setup = sem("index_ready"), sem("dve_setup")
        pe_wc, pe_gram, pe_wg = sem("pe_wc"), sem("pe_gram"), sem("pe_wg")
        wc_ready, wg_ready, gram_ready, half_ready = (
            sem(n) for n in ("wc_ready", "wg_ready", "gram_ready", "half_ready"))
        wt_ready, bias_ready, mix_ready, ones_ready, eps_ready = (
            sem(n) for n in ("wt_ready", "bias_ready", "mix_ready", "ones_ready", "eps_ready"))
        cleared, items_one, zx_clear = sem("cleared"), sem("items_one"), sem("zx_clear")
        pe_x, x_agg, x_root, xn_ready, pe_xt, xt_ready, pe_sumx, sumx_ready, pe_d1, d1_ready = (
            sem(n) for n in ("pe_x", "x_agg", "x_root", "xn_ready", "pe_xt", "xt_ready",
                             "pe_sumx", "sumx_ready", "pe_d1", "d1_ready"))
        pe_wx, scale_ready, we_hi_ready, wx_hi_ready, we_ready = (
            sem(n) for n in ("pe_wx", "scale_ready", "we_hi_ready", "wx_hi_ready", "we_ready"))
        tr_done, et_copied, eg_done, prod_done, ss_done, var_done, sd_done, rs_done, e_scaled = (
            sem(n) for n in ("tr_done", "et_copied", "eg_done", "prod_done", "ss_done", "var_done",
                             "sd_done", "rs_done", "e_scaled"))
        u_done, u_high, u_split, y_done, sq_done, ss2_done, sd2_done, rs2_done, y_normed = (
            sem(n) for n in ("u_done", "u_high", "u_split", "y_done", "sq_done", "ss2_done",
                             "sd2_done", "rs2_done", "y_normed"))
        x_placed, gr_done, gr_copied, merged, moved_dve, moved_act, z_high, z_split = (
            sem(n) for n in ("x_placed", "gr_done", "gr_copied", "merged", "moved_dve", "moved_act", "z_high",
                             "z_split"))
        fin_done, o_agg, o_root, o_recip, z_ready, zt_done, h0_ready, h0_ready_dve = (
            sem(n) for n in ("fin_done", "o_agg", "o_root", "o_recip", "z_ready", "zt_done",
                             "h0_ready", "h0_ready_dve"))
        h1_done, h1_added, h1_ready, h2_done, h2_ready, y_done_pe, y_ready, stored = (
            sem(n) for n in ("h1_done", "h1_added", "h1_ready", "h2_done", "h2_ready", "y_done_pe",
                             "y_ready", "stored"))

        def wait(eng, s, value):
            if not isinstance(value, int) or value > 0:
                eng.wait_ge(s, value)

        def group_rows(b, span):
            return z_s[PROJ * b:PROJ * b + PROJ, :, :].rearrange(
                "p (h g) j -> p h g j", h=2)[:, :, span[0]:span[1], :]

        def moved(rows, b, span):
            return z_q[rows, :, :].rearrange("p j (h g b) -> p h g j b", h=2, b=4)[
                :, :, span[0]:span[1], :, b]

        def move_columns(copy, b, jj, span):
            return copy(moved(slice(PROJ * jj, PROJ * jj + PROJ), b, span)[:, :, :, 0:JX],
                        group_rows(b, span)[:, :, :, 2 + JX * jj:2 + JX * jj + JX])

        block = ctx.enter_context(nc.Block())

        @block.sync
        def _(sp):
            def load(signal, *what):
                for dst, name in what:
                    sp.dma_start(dst, a[name]).then_inc(signal, 16)

            load(ids_in, (rows_in[:, :], "rows_in"))
            load(x_in, (dense_wd[:, :, :], "dense_wd"))
            load(w1_in, (w1_dense[:, :, :], "w1_dense"), (biases[:, :], "biases"))
            sp.wait_ge(gathered[0], 16 * 2 * len(chunk_pairs(0)))
            load(wl_in, (fold[:, :], "fold"), (second[:, :], "second"), (wl[:, :, :], "wl"))
            sp.wait_ge(gathered[2], 16 * 2 * len(chunk_pairs(2)))
            load(mlp_in, (w1[:, :, :], "w1"), (w2_w3[:, :], "w2_w3"))
            sp.wait_ge(y_ready, 2)
            sp.dma_start(out, y_row[:, :]).then_inc(stored, 16)
            sp.wait_ge(stored, 16)

        @block.gpsimd
        def _(pool):
            pool.memset(mix[:, :, :], 0.0).then_inc(cleared, 1)
            pool.memset(bias_l[:, :].bitcast(F32), 0.0).then_inc(cleared, 1)
            pool.memset(bias_r[:, :, :].bitcast(F32), 0.0).then_inc(cleared, 1)
            pool.memset(items[:, :, :, :, 0:1], 1.0).then_inc(items_one, 1)
            pool.memset(z_q[:, JX, :], 0.0).then_inc(cleared, 1)
            pool.wait_ge(cleared, 4)
            pool.memset(z_q[ROW_ONE:ROW_ONE + 1, JX, :], 1.0).then_inc(zx_clear, 1)
            pool.wait_ge(zx_clear, 1)
            pool.wait_ge(ids_in, 16)

            def span(c):
                return 2 * chunk_pairs(c)[0], 2 * len(chunk_pairs(c))

            def indices(k, c):
                lo, n = span(c)
                wait(pool, gathered[c], 16 * n * k)
                pool.tensor_tensor(index[:, lo:lo + n], ids[:, bass.ds(k * 2 * PAIRS + lo, n)],
                                   base[:, lo:lo + n], ALU.add).then_inc(index_ready, 1)

            def gathers(k, c):
                lo, n = span(c)
                wait(pool, u_done, CHUNKS * (k - 1) + c + 1)
                pool.wait_ge(index_ready, CHUNKS * k + c + 1)
                indices(*((k, c + 1) if c + 1 < CHUNKS else (k + 1, 0)))
                for t in range(lo, lo + n):
                    pool.indirect_dma_start(
                        e[:, t, :], None, a["table"],
                        bass.IndirectOffsetOnAxis(ap=index[:, t:t + 1], axis=0),
                    ).then_inc(gathered[c], 16)

            def tile(k):
                for c in range(CHUNKS):
                    gathers(k, c)

            indices(0, 0)
            tile(0)
            with pool.Fori(1, TILES) as k:
                tile(k)

        @block.tensor
        def _(pe):
            def transposes(k, c):
                wait(pe, gathered[c], 16 * 2 * len(chunk_pairs(c)) * (k + 1))
                wait(pe, et_copied, CHUNKS * k + c)
                for n, s in enumerate(chunk_pairs(c)):
                    last = pe.transpose(p_tr[:, n * P:(n + 1) * P],
                                        e[:, 2 * s:2 * s + 2, :].rearrange("p h d -> p (h d)"),
                                        ident[:, :])
                last.then_inc(tr_done, 1)

            def e_gram(k, c):
                q = CHUNKS * k + c
                wait(pe, et_copied, q + 1)
                wait(pe, prod_done, q)
                for n, s in enumerate(chunk_pairs(c)):
                    last = pe.matmul(p_eg[:, n * P:(n + 1) * P], e_t[:, c % 2, n * P:(n + 1) * P],
                                     gram_w[:, :], start=True, stop=True)
                last.then_inc(eg_done, 1)

            def fields(k, c):
                q = CHUNKS * k + c
                wait(pe, e_scaled, q + 1)
                wait(pe, u_split, q - 1)
                for s in chunk_pairs(c):
                    lo, hi = touched(s)
                    for bk in range(lo // CB, hi // CB + 1):
                        b0, b1_ = max(lo, bk * CB), min(hi, bk * CB + CB - 1)
                        if bk > c:
                            wait(pe, u_split, q)
                        for h in range(2):
                            last = pe.matmul(
                                p_u[bk % 2][HALF * h:HALF * h + HALF,
                                            (b0 - bk * CB) * PROJ:(b1_ + 1 - bk * CB) * PROJ],
                                e[:, 2 * s + h, :],
                                wt[:, s, b0 - lo:b1_ + 1 - lo, :].rearrange("p b j -> p (b j)"),
                                start=b0 == bk * CB and P * s <= bk * CB * FIELDS,
                                stop=b1_ == bk * CB + CB - 1, skip_group_check=True)
                last.then_inc(u_done, 1)

            def project(k, c):
                q = CHUNKS * k + c
                for h in range(2):
                    wait(pe, y_normed, 2 * (q - 1) + h + 1)
                    pe.matmul(p_y[:, h, :], bias_l[:, :],
                              bias_r[:, :, :].rearrange("p b j -> p (b j)"), start=True, stop=False)
                    if h == 0:
                        wait(pe, u_high, q + 1)
                    pe.matmul(p_y[:, h, :], wg_hi[:, h, :], u_hi[:, c % 2, :], start=False, stop=False)
                    pe.matmul(p_y[:, h, :], wg_lo[:, h, :], u_hi[:, c % 2, :], start=False, stop=False)
                    if h == 0:
                        wait(pe, u_split, q + 1)
                    pe.matmul(p_y[:, h, :], wg_hi[:, h, :], u_lo[:, c % 2, :], start=False,
                              stop=True).then_inc(y_done, 1)

            def sample_gram(k, c):
                q = CHUNKS * k + c
                wait(pe, y_normed, 2 * q + 2)
                wait(pe, x_placed, q + 1)
                wait(pe, gr_copied, q)
                for h in range(2):
                    for g in range(CG):
                        at = (h * CG + g) * ITEM
                        for b in range(4):
                            it = items[:, c, h, 4 * g + b, :]
                            last = pe.matmul(p_gr[PROJ * b:PROJ * b + PROJ, at:at + ITEM],
                                             it[:, 2:ITEM], it[:, :], start=True, stop=True)
                last.then_inc(gr_done, 1)

            def interact(k, part):
                if part == 0:
                    pe.wait_ge(we_ready, 1)
                    if isinstance(k, int) and k == TILES - 1:
                        pe.wait_ge(z_ready, k)
                js = Z_PARTS[part]
                pe.wait_ge(z_high, 2 * k + part + 1)
                for j in js:
                    pe.matmul(p_o[:, :], z_hi[:, j, :], we_hi[:, j, :], start=(j == 0), stop=False)
                    pe.matmul(p_o[:, :], z_hi[:, j, :], we_lo[:, j, :], start=False, stop=False)
                wait(pe, z_split, 2 * k + part + 1)
                for j in js:
                    last = pe.matmul(p_o[:, :], z_lo[:, j, :], we_hi[:, j, :], start=False,
                                     stop=(j == KX - 1))
                if part == len(Z_PARTS) - 1:
                    last.then_inc(fin_done, 1)

            def turn_z(k, banks=(p_o,) * (KEPT // P)):
                wait(pe, z_ready, k + 1)
                for n in range(KEPT // P):
                    last = pe.transpose(banks[n][:, n * P:(n + 1) * P], z[:, n * P:(n + 1) * P], ident[:, :])
                last.then_inc(zt_done, 1)

            def hidden1(k, bank=p_o, units=range(HID1 // P), signal=True,
                        onto_dense=False):
                wait(pe, h0_ready, k + 1)
                if isinstance(k, int) and k == TILES - 1:
                    pe.wait_ge(h0_ready_dve, 1)
                for m in units:
                    for n in range(KEPT // P):
                        last = pe.matmul(bank[:, m * P:(m + 1) * P], w1[:, n, m * P:(m + 1) * P],
                                         h0[:, n, :], start=(n == 0 and not onto_dense),
                                         stop=(n == KEPT // P - 1), skip_group_check=onto_dense)
                if signal:
                    last.then_inc(h1_done, 1)

            def hidden2(k, bank=p_o):
                wait(pe, h1_ready, k + 1)
                for m in range(HID2 // P):
                    for n in range(HID1 // P):
                        last = pe.matmul(bank[:, m * P:(m + 1) * P], w2[:, n, m * P:(m + 1) * P],
                                         h1[:, n, :], start=(n == 0), stop=(n == HID1 // P - 1))
                last.then_inc(h2_done, 1)

            def dense_first(k):
                pe.wait_ge(gr_copied, CHUNKS * TILES)
                for units, bank in zip(UNIT_HALVES, last_h1):
                    ms = slice(units[0], units[-1] + 1)
                    pe.matmul(bank.rearrange("p (m b) -> p m b", b=P)[:, ms, :], ident[:, :],
                              d1[:, ms, k * P:(k + 1) * P], start=True, stop=False, skip_group_check=True)

            def last_hidden2(k):
                for half, ns in enumerate(UNIT_HALVES):
                    pe.wait_ge(h1_ready, k + 1 + half)
                    for m in range(HID2 // P):
                        for n in ns:
                            last = pe.matmul(p_u[m][:, 0:P], w2[:, n, m * P:(m + 1) * P], h1[:, n, :],
                                             start=(n == 0), stop=(n == HID1 // P - 1))
                        if half == 1:
                            last.then_inc(h2_done, 1)

            def result(bank, samples, signal=True):
                for n in range(HID2 // P):
                    last = pe.matmul(bank[0:1, samples], w3[:, n:n + 1], h2[:, n, samples],
                                     start=(n == 0), stop=(n == HID2 // P - 1))
                if signal:
                    last.then_inc(y_done_pe, 1)

            def x_product():
                pe.wait_ge(x_in, 16)
                for t in range(TILES):
                    for n in range(2):
                        last = pe.matmul(p_o[:, t * EMB:(t + 1) * EMB],
                                         dense_t[:, n, t * P:(t + 1) * P], wd[:, n, :],
                                         start=(n == 0), stop=(n == 1))
                last.then_inc(pe_x, 1)

            def x_turn():
                pe.wait_ge(xn_ready, 1)
                for t in range(TILES):
                    last = pe.transpose(p_o[:, t * P:(t + 1) * P], xn[:, t, :], ident[:, :])
                last.then_inc(pe_xt, 1)

            def x_sum():
                pe.wait_ge(xt_ready, 1)
                pe.wait_ge(ones_ready, 1)
                pe.matmul(p_o[ROW_SUMX:ROW_SUMX + 1, :], ones[:, :], x_t[:, :], start=True,
                          stop=True).then_inc(pe_sumx, 1)

            def dense_hidden(m):
                pe.wait_ge(w1_in, 32)
                if m == DENSE_BANKS:
                    pe.wait_ge(d1_ready, 1)
                for n in range(DENSE // P):
                    last = pe.matmul(p_d[m % DENSE_BANKS], w1_dense[:, n, m * P:(m + 1) * P],
                                     dense_t[:, n, :], start=(n == 0), stop=(n == DENSE // P - 1))
                last.then_inc(pe_d1, 1)

            def extra_weights(js):
                pe.wait_ge(mix_ready, 1)
                pe.wait_ge(wl_in, 48)
                pe.wait_ge(sumx_ready, 1)
                for j in js:
                    last = pe.matmul(p_o[:, :], mix[:, j, :], wl[:, j, :], start=(j == 0),
                                     stop=(j == KX - 1))
                if j == KX - 1:
                    last.then_inc(pe_wx, 1)

            pe.wait_ge(ws_in, 16)
            pe.matmul(p_o[:, 0:P], center[:, :], ws[:, :].unsqueeze(1).to_broadcast([EMB, 2, DIM]),
                      start=True, stop=True).then_inc(pe_wc, 1)
            pe.wait_ge(wc_ready, 1)
            pe.matmul(p_gr[:, 0:P], wc[:, :, :].rearrange("p h d -> p (h d)"),
                      wc[:, :, :].rearrange("p h d -> p (h d)"), start=True, stop=True).then_inc(pe_gram, 1)
            pe.wait_ge(wg_ready, 1)
            pe.transpose(p_o[:, 0:P], wg[:, :, :].rearrange("p h d -> p (h d)"),
                         ident[:, :]).then_inc(pe_wg, 1)
            pe.wait_ge(half_ready, 1)
            x_product()

            dense_hidden(0)
            dense_hidden(1)
            transposes(0, 0)
            x_turn()
            for c in range(CHUNKS):
                e_gram(0, c)
                if c == 0:
                    dense_hidden(2)
                    dense_hidden(3)
                    transposes(0, 1)
                    pe.wait_ge(wt_ready, 1)
                else:
                    if c == 1:
                        pe.wait_ge(bias_ready, 1)
                        pe.wait_ge(d1_ready, HID1 // P)
                        x_sum()
                    if c == 2:
                        extra_weights(Z_PARTS[1])
                    project(0, c - 1)
                    if c >= 2:
                        pe.wait_ge(items_one, 1)
                        sample_gram(0, c - 2)
                    transposes(*after(0, c))
                fields(0, c)
                if c == 1:
                    extra_weights(Z_PARTS[0])

            pe.wait_ge(mlp_in, 32)

            def round_(k, c, z):
                turn_first = z is not None and c in TURN_FIRST
                e_gram(k, c)
                if turn_first:
                    transposes(*after(k, c))
                if z is not None:
                    if c == 0:
                        interact(z, 1)
                    if c == 1:
                        hidden1(z)
                    if c == 2:
                        hidden2(z)
                project(*before(k, c, 1))
                sample_gram(*before(k, c, 2))
                if z is not None and c == 3:
                    interact(z, 0)
                if not turn_first and not is_last(k, c):
                    transposes(*after(k, c))
                fields(k, c)
                if z is not None and c == 0:
                    turn_z(z)

            for c in range(3):
                round_(1, c, None)
            with pe.Fori(1, TILES - 1) as k:
                round_(k, 3, k - 1)
                for c in range(3):
                    round_(k + 1, c, k - 1)
            k = TILES - 1
            round_(k, 3, k - 1)
            interact(k - 1, 1)
            project(k, CHUNKS - 1)
            turn_z(k - 1, (last_tr,) * (KEPT // P))
            sample_gram(k, CHUNKS - 2)
            hidden1(k - 1, last_h, UNIT_HALVES[0], signal=False)
            sample_gram(k, CHUNKS - 1)
            hidden1(k - 1, last_h, UNIT_HALVES[1])
            dense_first(k)
            pe.wait_ge(h2_ready, k - 1)
            result(last_y, slice(0, (k - 1) * P), signal=False)
            for part in range(len(Z_PARTS)):
                interact(k, part)
            hidden2(k - 1, last_tr)
            turn_z(k, (p_o,) * (KEPT // P - 1) + (last_z,))
            pe.wait_ge(h2_ready, k)
            result(last_y, slice((k - 1) * P, k * P))
            for units, bank in zip(UNIT_HALVES, last_h1):
                hidden1(k, bank, units, onto_dense=True)
            last_hidden2(k)
            pe.wait_ge(h2_ready, k + 1)
            result(p_o, slice(k * P, BATCH))

        @block.vector
        def _(dve):
            count = [0]

            def link(ins):
                count[0] += 1
                ins.then_inc(dve_setup, 1)
                dve.wait_ge(dve_setup, count[0])

            def bcast(ap, n):
                return ap.unsqueeze(2).to_broadcast([ap.shape[0], ap.shape[1], n])

            dve.memset(eps[:, :], EPS).then_inc(eps_ready, 1)
            dve.memset(ones[:, :], 1.0).then_inc(ones_ready, 1)
            link(dve.memset(gram_w[:, :], 0.0))
            link(dve.memset(wg_hi[:, :, :].bitcast(F32), 0.0))
            link(dve.memset(wg_lo[:, :, :].bitcast(F32), 0.0))
            dve.wait_ge(pe_wc, 1)
            dve.tensor_copy(wc[:, :, :].rearrange("p h d -> p (h d)"), p_o[:, 0:P]).then_inc(wc_ready, 1)
            dve.tensor_scalar(wg[:, :, :].rearrange("p h d -> p (h d)"), p_o[:, 0:P], gs[:, 0:1], None,
                              ALU.mult).then_inc(wg_ready, 1)
            dve.wait_ge(pe_gram, 1)
            for h in range(2):
                r = slice(DIM * h, DIM * h + DIM)
                last = dve.tensor_copy(gram_w[r, r], p_gr[r, r])
            last.then_inc(gram_ready, 1)
            dve.wait_ge(pe_wg, 1)
            for h in range(2):
                r = slice(DIM * h, DIM * h + DIM)
                link(dve.tensor_copy(wg_hi[r, h, :], p_o[r, 0:P]))
                last = dve.tensor_tensor(wg_lo[r, h, :], p_o[r, 0:P], wg_hi[r, h, :].bitcast(F32),
                                         ALU.subtract)
            last.then_inc(half_ready, 1)
            dve.wait_ge(wsi_in, 16)
            link(dve.tensor_reduce(wsi_mean[:, :], wsi[:, :, :], AX_X, ALU.add))
            link(dve.tensor_scalar(wsi_mean[:, :], wsi_mean[:, :], 1.0 / PROJ, None, ALU.mult))
            link(dve.tensor_tensor(wsi[:, :, :], wsi[:, :, :], bcast(wsi_mean[:, :], PROJ), ALU.subtract))
            dve.tensor_tensor(
                wt[:, :, :, :], wsi[:, :, :].unsqueeze(2).to_broadcast([P, PAIRS, TOUCH, PROJ]),
                touch[:, :, :].unsqueeze(3).to_broadcast([P, PAIRS, TOUCH, PROJ]),
                ALU.mult).then_inc(wt_ready, 1)

            def x_norm():
                dve.wait_ge(pe_x, 1)
                for t in range(TILES):
                    last = dve.bn_stats(x_stats[:, t, :], p_o[:, t * EMB:(t + 1) * EMB])
                link(last)
                for t in range(TILES):
                    last = dve.bn_aggr(x_mv[:, t, :], x_stats[:, t, :])
                last.then_inc(x_agg, 1)
                dve.wait_ge(x_root, 1)
                link(dve.reciprocal(x_rs[:, :], x_sd[:, :]))
                for t in range(TILES):
                    last = dve.tensor_scalar(xn[:, t, :], p_o[:, t * EMB:(t + 1) * EMB],
                                             x_mv[:, t, 0:1], x_rs[:, t:t + 1], ALU.subtract, ALU.mult)
                last.then_inc(xn_ready, 1)

            def bias_parts(value, n, masks, dst):
                hi = split_h[:, 0:n]
                link(dve.tensor_copy(hi, value))
                link(dve.tensor_tensor(split_r[:, 0:n], value, hi.bitcast(F32), ALU.subtract))
                link(dve.tensor_scalar(split_t[:, 0:n], hi.bitcast(F32), part4[:, masks:masks + 1],
                                       None, ALU.mult))
                link(dve.scalar_tensor_tensor(dst, split_r[:, 0:n], part4[:, masks + 1:masks + 2],
                                              split_t[:, 0:n], ALU.mult, ALU.add))

            def bias_first():
                dve.wait_ge(bias_in, 16)
                dve.wait_ge(cleared, 4)
                link(dve.tensor_reduce(wsum4[:, :], wsi4[:, :, :], AX_X, ALU.add))
                link(dve.tensor_reduce(wmean4[:, :], wsum4[:, :], AX_X, ALU.add))
                link(dve.tensor_scalar(wmean4[:, :], wmean4[:, :], 1.0 / PROJ, None, ALU.mult))
                link(dve.tensor_scalar(wsum4[:, :], wsum4[:, :], wmean4[:, 0:1], None, ALU.subtract))
                bias_parts(bs4[:, :], EMB, 0, bias_l[0:PARTS ** 2, :])

            def bias_second():
                bias_parts(wsum4[:, :], PROJ, PARTS, bias_w[:, :])
                dve.tensor_copy(bias_r[0:PARTS ** 2, :, :], bias_w[:, :].unsqueeze(1).to_broadcast(
                    [PARTS ** 2, CB, PROJ])).then_inc(bias_ready, 1)

            def mixing():
                dve.wait_ge(wl_in, 48)
                dve.wait_ge(cleared, 4)
                dve.tensor_scalar(scale_w[:, :], g_c, g_i, None, ALU.mult).then_inc(scale_ready, 1)
                dve.tensor_scalar(mix[:, 0:JX, 0:PROJ], is_col, b_i, None, ALU.mult)
                link(dve.tensor_tensor(mix_t[:, :, :], is_row.unsqueeze(1).to_broadcast([P, JX, PROJ]),
                                       bcast(b_c, PROJ), ALU.mult))
                link(dve.tensor_tensor(mix[:, 0:JX, 0:PROJ], mix[:, 0:JX, 0:PROJ], mix_t[:, :, :], ALU.add))
                dve.tensor_scalar(mix[:, 0:JX, ROW_ONE], b_c, b_i, float(EMB), ALU.mult, ALU.mult)
                mine = slice(ROW_X, ROW_X + PROJ)
                dve.tensor_copy(mix[mine, JX, mine], is_row[mine, :])
                dve.tensor_copy(mix[mine, JX, ROW_SUMX:ROW_SUMX + 1], b_i[mine, :]).then_inc(mix_ready, 1)

            def weights_low(js):
                dve.wait_ge(scale_ready, 1)
                for j in js:
                    dve.wait_ge(we_hi_ready, j + 1)
                    dve.scalar_tensor_tensor(we_lo[:, j, :], wl[:, j, :], scale_w[:, j:j + 1],
                                             we_hi[:, j, :].bitcast(F32), ALU.mult, ALU.subtract)

            def last_weights_low():
                dve.wait_ge(wx_hi_ready, 1)
                dve.scalar_tensor_tensor(we_lo[:, JX, :], p_o[:, :], row_scale[:, 0:1],
                                         we_hi[:, JX, :].bitcast(F32), ALU.mult,
                                         ALU.subtract).then_inc(we_ready, 1)

            def rows_sum(k, c):
                q = CHUNKS * k + c
                pairs = chunk_pairs(c)
                n, at = 2 * len(pairs), 2 * pairs[0]
                dve.wait_ge(eg_done, q + 1)
                dve.tensor_tensor(prod[:, 0:n * DIM], e[:, at:at + n, :].rearrange("p t d -> p (t d)"),
                                  p_eg[:, 0:n * DIM], ALU.mult).then_inc(prod_done, 1)
                dve.wait_ge(prod_done, q + 1)
                dve.tensor_reduce(ss[:, 0:n], prod[:, 0:n * DIM].rearrange("p (t d) -> p t d", d=DIM),
                                  AX_X, ALU.add).then_inc(ss_done, 1)
                dve.wait_ge(ss_done, q + 1)
                dve.tensor_scalar(var[:, 0:n], ss[:, 0:n], 1.0 / EMB, 0.0, ALU.mult,
                                  ALU.max).then_inc(var_done, 1)

            def rows_scale(k, c):
                q = CHUNKS * k + c
                pairs = chunk_pairs(c)
                n, at = 2 * len(pairs), 2 * pairs[0]
                dve.wait_ge(sd_done, q + 1)
                dve.reciprocal(rs[:, 0:n], sd[:, 0:n]).then_inc(rs_done, 1)
                dve.wait_ge(rs_done, q + 1)
                dve.tensor_tensor(e[:, at:at + n, :], e[:, at:at + n, :], bcast(rs[:, 0:n], DIM),
                                  ALU.mult).then_inc(e_scaled, 1)

            def norm_sum(k, c, h):
                q = CHUNKS * k + c
                dve.wait_ge(sq_done, 2 * q + h + 1)
                dve.tensor_reduce(ss2[:, h, :], sq[:, h, :].rearrange("p (b j) -> p b j", j=PROJ),
                                  AX_X, ALU.add).then_inc(ss2_done, 1)

            def norm_scale(k, c):
                q = CHUNKS * k + c
                dve.wait_ge(sd2_done, q + 1)
                dve.reciprocal(rs2[:, :, :], sd2[:, :, :]).then_inc(rs2_done, 1)
                wait(dve, gr_done, q - CHUNKS + 1)
                dve.wait_ge(rs2_done, q + 1)
                for h in range(2):
                    dve.tensor_tensor(items[:, c, h, :, 2:ITEM],
                                      p_y[:, h, :].rearrange("p (b j) -> p b j", j=PROJ),
                                      bcast(rs2[:, h, :], PROJ), ALU.mult).then_inc(y_normed, 1)

            def low_u(k, c):
                q = CHUNKS * k + c
                dve.wait_ge(u_high, q + 1)
                dve.tensor_tensor(u_lo[:, c % 2, :], p_u[c % 2][:, :], u_hi[:, c % 2, :].bitcast(F32),
                                  ALU.subtract).then_inc(u_split, 1)

            def merge(k, span=ALL_GROUPS):
                late = span[1] == ALL_GROUPS[1]
                dve.wait_ge(gr_copied, CHUNKS * k + CHUNKS - (0 if late else 1))
                wait(dve, z_high, 2 * k)
                dve.tensor_copy(moved(slice(0, PROJ), 0, span)[:, :, :, JX],
                                group_rows(0, span)[:, :, :, 0])
                blocks = z_s[:, :, :].rearrange("p (h g) j -> p h g j", h=2)[:, :, span[0]:span[1], :]
                dve.copy_predicated(
                    blocks[:, :, :, 2:2 + BLOCKS],
                    second[:, :].unsqueeze(1).unsqueeze(1).to_broadcast([P, 2, span[1] - span[0], BLOCKS]),
                    blocks[:, :, :, 2 + BLOCKS:ITEM]).then_inc(merged, 1)

            def move(k, quadrants, span=ALL_GROUPS, n=1):
                dve.wait_ge(merged, k + n)
                for b in range(4):
                    if b > 0:
                        dve.tensor_copy(moved(slice(0, PROJ), b, span)[:, :, :, JX],
                                        group_rows(b, span)[:, :, :, 0])
                    for jj in quadrants:
                        last = move_columns(dve.tensor_copy, b, jj, span)
                last.then_inc(moved_dve, 1)

            def low_z(k, part):
                dve.wait_ge(z_high, 2 * k + part + 1)
                js = slice(Z_PARTS[part][0], Z_PARTS[part][-1] + 1)
                dve.tensor_tensor(z_lo[:, js, :], z_q[:, js, :], z_hi[:, js, :].bitcast(F32),
                                  ALU.subtract).then_inc(z_split, 1)

            def out_stats(k):
                dve.wait_ge(fin_done, k + 1)
                dve.bn_stats(o_stats[:, :], p_o[:, :])
                dve.drain()
                dve.bn_aggr(o_mv[:, :], o_stats[:, :]).then_inc(o_agg, 1)

            def out_scale(k):
                dve.wait_ge(o_root, k + 1)
                dve.reciprocal(o_rs[:, :], o_sd[:, :]).then_inc(o_recip, 1)
                dve.wait_ge(o_recip, k + 1)
                dve.tensor_scalar(z[:, :], p_o[:, 0:KEPT], o_mv[:, 0:1], o_rs[:, 0:1], ALU.subtract,
                                  ALU.mult).then_inc(z_ready, 1)

            def add_dense(k, bank=p_o):
                dve.wait_ge(h1_done, k + 1)
                dve.tensor_tensor(h1_sum[:, :, :], bank[:, :].rearrange("p (m b) -> p m b", b=P),
                                  d1[:, :, bass.ds(k * P, P)], ALU.add).then_inc(h1_added, 1)

            def gain_last_z(k):
                dve.wait_ge(w1_in, 32)
                dve.wait_ge(zt_done, k + 1)
                n = KEPT // P - 1
                dve.tensor_scalar(h0[:, n, :], last_z[:, n * P:(n + 1) * P], glb[:, 0, n:n + 1],
                                  glb[:, 1, n:n + 1], ALU.mult, ALU.add).then_inc(h0_ready_dve, 1)

            x_norm()
            bias_first()
            for c in range(CHUNKS):
                if c > 0:
                    low_u(0, c - 1)
                rows_sum(0, c)
                if c == 1:
                    mixing()
                rows_scale(0, c)
                if c == 2:
                    weights_low(range(2))
                if c == 0:
                    bias_second()
                else:
                    norm_sum(0, c - 1, 0)
                    norm_sum(0, c - 1, 1)
                    if c >= 2:
                        weights_low(range(c, c + 1))
                    norm_scale(0, c - 1)

            def round_(k, c, z):
                last = before(k, c, 1)
                if z is None or c != 1:
                    low_u(*last)
                rows_sum(k, c)
                if z is not None and c == 1:
                    low_u(*last)
                if z is not None and c == 3:
                    low_z(z, 0)
                rows_scale(k, c)
                if z is not None:
                    if c == 0:
                        out_stats(z)
                    if c == 1:
                        add_dense(z)
                norm_sum(*last, 0)
                if z is not None and c == 0:
                    out_scale(z)
                norm_sum(*last, 1)
                if c == 2:
                    move(k - 1, DVE_MOVES)
                if z is not None and c == 3:
                    low_z(z, 1)
                norm_scale(*last)
                if z is None and c == 0:
                    last_weights_low()
                if c == 1:
                    merge(k - 1)

            for c in range(3):
                round_(1, c, None)
            with dve.Fori(1, TILES - 1) as k:
                round_(k, 3, k - 1)
                for c in range(3):
                    round_(k + 1, c, k - 1)
            k = TILES - 1
            round_(k, 3, k - 1)
            low_u(k, CHUNKS - 1)
            out_stats(k - 1)
            out_scale(k - 1)
            norm_sum(k, CHUNKS - 1, 0)
            norm_sum(k, CHUNKS - 1, 1)
            norm_scale(k, CHUNKS - 1)
            merge(k, EARLY)
            move(k, EARLY_DVE_MOVES, EARLY, 1)
            merge(k, LATE)
            move(k, LATE_DVE_MOVES, LATE, 2)
            for part in range(len(Z_PARTS)):
                low_z(k, part)
            add_dense(k - 1, last_h)
            out_stats(k)
            out_scale(k)
            gain_last_z(k)

        @block.scalar
        def _(act):
            for signal, dst, name in ((ws_in, setup[:, :], "setup"), (wsi_in, wsi_touch[:, :, :], "wsi_touch"),
                                      (bias_in, bias4[:, :], "bias4")):
                act.dma_start(dst, a[name]).then_inc(signal, 16)

            def root(dst, src, scale):
                return act.activation(dst, src, ACT.Sqrt, bias=eps[0:dst.shape[0], 0:1], scale=scale)

            def copy_et(k, c):
                q = CHUNKS * k + c
                n = len(chunk_pairs(c)) * P
                act.wait_ge(tr_done, q + 1)
                wait(act, eg_done, q - 1)
                act.activation(e_t[:, c % 2, 0:n], p_tr[:, 0:n], ACT.Copy).then_inc(et_copied, 1)

            def row_root(k, c):
                q = CHUNKS * k + c
                n = 2 * len(chunk_pairs(c))
                act.wait_ge(var_done, q + 1)
                wait(act, rs_done, q)
                root(sd[:, 0:n], var[:, 0:n], 1.0).then_inc(sd_done, 1)

            def squares(k, c, h):
                q = CHUNKS * k + c
                act.wait_ge(y_done, 2 * q + h + 1)
                wait(act, ss2_done, 2 * (q - 1) + h + 1)
                act.activation(sq[:, h, :], p_y[:, h, :], ACT.Square).then_inc(sq_done, 1)

            def norm_roots(k, c):
                q = CHUNKS * k + c
                act.wait_ge(ss2_done, 2 * q + 2)
                wait(act, rs2_done, q)
                root(sd2[:, :, :], ss2[:, :, :], 1.0 / PROJ).then_inc(sd2_done, 1)

            def place_x(k, c):
                q = CHUNKS * k + c
                wait(act, gr_done, q - CHUNKS + 1)
                act.activation(items[:, c, :, :, 1],
                               x_t[:, bass.ds(k * P, P)].rearrange("p (h b) -> p h b", h=2)
                               [:, :, CB * c:CB * c + CB], ACT.Copy).then_inc(x_placed, 1)

            def high_u(k, c):
                q = CHUNKS * k + c
                act.wait_ge(u_done, q + 1)
                wait(act, y_done, 2 * (q - 1))
                act.activation(u_hi[:, c % 2, :], p_u[c % 2][:, :], ACT.Copy).then_inc(u_high, 1)

            def copy_gram(k, c):
                act.wait_ge(gr_done, CHUNKS * k + c + 1)
                wait(act, moved_dve, k)
                wait(act, moved_act, len(ACT_MOVES) * k)
                per_half = GROUPS // 2
                for h in range(2):
                    at = per_half * h + CG * c
                    last = act.activation(
                        z_s[:, at:at + CG, :],
                        p_gr[:, h * CG * ITEM:(h + 1) * CG * ITEM]
                        .rearrange("p (g j) -> p g j", j=ITEM), ACT.Copy)
                last.then_inc(gr_copied, 1)

            def move_x(k, span=ALL_GROUPS):
                late = span[1] == ALL_GROUPS[1]
                act.wait_ge(gr_copied, CHUNKS * k + CHUNKS - (0 if late else 1))
                wait(act, z_split, 2 * k)
                if late:
                    act.activation(z_q[ROW_SUMX:ROW_SUMX + 1, JX, :],
                                   sumx[ROW_SUMX:ROW_SUMX + 1, bass.ds(k * P, P)], ACT.Copy)
                for b in range(4):
                    act.copy(moved(slice(ROW_X, ROW_X + PROJ), b, span)[:, :, :, JX],
                             group_rows(b, span)[:, :, :, 1])

            def move(k, jj, span=ALL_GROUPS, n=1):
                act.wait_ge(merged, k + n)
                for b in range(4):
                    last = move_columns(act.copy, b, jj, span)
                last.then_inc(moved_act, 1)

            def high_z(k, part, act_moves=len(ACT_MOVES), dve_moves=1):
                act.wait_ge(moved_act, len(ACT_MOVES) * k + act_moves)
                act.wait_ge(moved_dve, k + dve_moves)
                js = slice(Z_PARTS[part][0], Z_PARTS[part][-1] + 1)
                act.activation(z_hi[:, js, :], z_q[:, js, :], ACT.Copy).then_inc(z_high, 1)

            def dense_bias(m):
                act.wait_ge(pe_d1, m + 1)
                act.wait_ge(w1_in, 32)
                act.activation(d1[:, m, :], p_d[m % DENSE_BANKS], ACT.Identity,
                               bias=b1[:, m:m + 1]).then_inc(d1_ready, 1)

            def out_root(k):
                act.wait_ge(o_agg, k + 1)
                root(o_sd[:, :], o_mv[:, 1:2], 1.0).then_inc(o_root, 1)

            def gain_z(k, bank=p_o, ns=range(KEPT // P)):
                act.wait_ge(zt_done, k + 1)
                for n in ns:
                    last = act.activation(h0[:, n, :], bank[:, n * P:(n + 1) * P], ACT.Identity,
                                          bias=glb[:, 1, n:n + 1], scale=glb[:, 0, n:n + 1])
                last.then_inc(h0_ready, 1)

            def relu1(k):
                act.wait_ge(h1_added, k + 1)
                act.activation(h1[:, :, :], h1_sum[:, :, :], ACT.Relu).then_inc(h1_ready, 1)

            def relu2(k, bank=p_o):
                act.wait_ge(h2_done, k + 1)
                for n in range(HID2 // P):
                    last = act.activation(h2[:, n, bass.ds(k * P, P)], bank[:, n * P:(n + 1) * P],
                                          ACT.Relu, bias=b2[:, n:n + 1])
                last.then_inc(h2_ready, 1)

            def last_relu1(k):
                for n, (units, bank) in enumerate(zip(UNIT_HALVES, last_h1)):
                    act.wait_ge(h1_done, k + 1 + n)
                    ms = slice(units[0], units[-1] + 1)
                    act.activation(h1[:, ms, :], bank.rearrange("p (m b) -> p m b", b=P)[:, ms, :],
                                   ACT.Relu).then_inc(h1_ready, 1)

            def last_relu2(k):
                for n in range(HID2 // P):
                    act.wait_ge(h2_done, k + 1 + n)
                    last = act.activation(h2[:, n, k * P:(k + 1) * P], p_u[n][:, 0:P], ACT.Relu,
                                          bias=b2[:, n:n + 1])
                last.then_inc(h2_ready, 1)

            def copy_y(bank, samples, n):
                act.wait_ge(y_done_pe, n)
                act.activation(y_row[:, samples], bank[0:1, samples], ACT.Copy).then_inc(y_ready, 1)

            def high_weights(js):
                act.wait_ge(scale_ready, 1)
                for j in js:
                    act.activation(we_hi[:, j, :], wl[:, j, :], ACT.Copy,
                                   scale=scale_w[:, j:j + 1]).then_inc(we_hi_ready, 1)

            act.wait_ge(eps_ready, 1)
            root(warm[:, :], eps[:, :], 1.0)
            act.wait_ge(x_agg, 1)
            root(x_sd[:, :], x_mv[:, :, 1], 1.0).then_inc(x_root, 1)
            dense_bias(0)
            copy_et(0, 0)
            for c in range(CHUNKS):
                if c > 0:
                    high_u(0, c - 1)
                    if c == 2:
                        high_weights(range(2))
                else:
                    dense_bias(1)
                row_root(0, c)
                if c >= 2:
                    high_weights(range(c, c + 1))
                if c == 0:
                    act.wait_ge(pe_xt, 1)
                    act.activation(x_t[:, :], p_o[:, :], ACT.Identity, bias=gdb[:, 1:2],
                                   scale=gdb[:, 0:1]).then_inc(xt_ready, 1)
                    act.wait_ge(xt_ready, 1)
                    dense_bias(2)
                    dense_bias(3)
                    copy_et(0, 1)
                else:
                    if c == 1:
                        act.wait_ge(pe_sumx, 1)
                        act.activation(sumx[ROW_SUMX:ROW_SUMX + 1, :], p_o[ROW_SUMX:ROW_SUMX + 1, :],
                                       ACT.Copy).then_inc(sumx_ready, 1)
                    squares(0, c - 1, 0)
                    squares(0, c - 1, 1)
                    copy_et(*after(0, c))
                    norm_roots(0, c - 1)
                    if c >= 2:
                        copy_gram(0, c - 2)
                place_x(0, c)
            act.wait_ge(pe_wx, 1)
            act.activation(we_hi[:, JX, :], p_o[:, :], ACT.Copy,
                           scale=row_scale[:, 0:1]).then_inc(wx_hi_ready, 1)
            act.wait_ge(zx_clear, 1)
            act.wait_ge(mlp_in, 32)
            act.wait_ge(sumx_ready, 1)

            def round_(k, c, z):
                turn_first = z is not None and c in TURN_FIRST
                last = before(k, c, 1)
                high_u(*last)
                if turn_first:
                    copy_et(*after(k, c))
                if c == 2:
                    move(k - 1, 1)
                    move(k - 1, 2)
                row_root(k, c)
                if z is not None and c == 3:
                    high_z(z, 0)
                    high_z(z, 1)
                squares(*last, 0)
                squares(*last, 1)
                if c == 2:
                    move(k - 1, 3)
                if z is not None and c == 0:
                    out_root(z)
                if not turn_first and not is_last(k, c):
                    copy_et(*after(k, c))
                norm_roots(*last)
                if z is not None:
                    if c == 0:
                        gain_z(z)
                    if c == 1:
                        relu1(z)
                place_x(k, c)
                copy_gram(*before(k, c, 2))
                if c == 1:
                    move_x(k - 1)
                if z is not None and c == 2:
                    relu2(z)

            for c in range(3):
                round_(1, c, None)
            with act.Fori(1, TILES - 1) as k:
                round_(k, 3, k - 1)
                for c in range(3):
                    round_(k + 1, c, k - 1)
            k = TILES - 1
            round_(k, 3, k - 1)
            high_u(k, CHUNKS - 1)
            out_root(k - 1)
            squares(k, CHUNKS - 1, 0)
            squares(k, CHUNKS - 1, 1)
            gain_z(k - 1, last_tr)
            norm_roots(k, CHUNKS - 1)
            copy_gram(k, CHUNKS - 2)
            move_x(k, EARLY)
            move(k, EARLY_ACT_MOVES[0], EARLY, 1)
            copy_gram(k, CHUNKS - 1)
            move(k, EARLY_ACT_MOVES[1], EARLY, 1)
            move_x(k, LATE)
            for jj in LATE_ACT_MOVES:
                move(k, jj, LATE, 2)
            for part in range(len(Z_PARTS)):
                high_z(k, part, len(EARLY_ACT_MOVES) + len(LATE_ACT_MOVES), 2)
            relu1(k - 1)
            out_root(k)
            relu2(k - 1, last_tr)
            gain_z(k, ns=range(KEPT // P - 1))
            copy_y(last_y, slice(0, k * P), 1)
            last_relu1(k)
            last_relu2(k)
            copy_y(p_o, slice(k * P, BATCH), 2)


def is_last(k, c):
    return isinstance(k, int) and (k, c) == (TILES - 1, CHUNKS - 1)


def after(k, c):
    return (k, c + 1) if c < CHUNKS - 1 else (k + 1, 0)


def before(k, c, n):
    return (k, c - n) if c >= n else (k - 1, c - n + CHUNKS)


def kernel(**inputs):
    import numpy as np
    import concourse.bacc as bacc
    from concourse.bass_utils import run_bass_kernel_spmd

    def arr(name):
        return np.asarray(inputs[name])

    tables = [arr(f"tbl_{f}") for f in range(FIELDS)]
    starts = np.concatenate([[0], np.cumsum([t.shape[0] for t in tables])[:-1]]).astype(np.int32)
    rows = np.arange(PAIRS * P).reshape(PAIRS, P)
    field, sample = rows % FIELDS, rows // FIELDS
    part = np.arange(P)
    row_i, quad = part % PROJ, part // PROJ
    past = (row_i[:, None] - JX * quad[:, None] - np.arange(JX)) % PROJ
    col = JX * quad[:, None] + np.arange(JX) + BLOCKS * ((past == 0) | (past > BLOCKS))
    high, low = np.maximum(row_i[:, None], col) + 1, np.minimum(row_i[:, None], col) + 1
    wl_t = arr("L0_rec_Wl").T
    wl_pairs = np.where((past > 0)[:, :, None], wl_t[np.where(past > 0, high * (high - 1) // 2 + low, 0)],
                        np.float32(0))
    has_x = (part >= ROW_X) & (part < ROW_X + PROJ)
    wl_x = np.where(has_x[:, None], wl_t[(row_i + 1) * row_i // 2], np.float32(0))
    past_block = (row_i[:, None] - np.arange(BLOCKS)) % PROJ
    gsi, bsi = arr("L0_rec_gsi"), arr("L0_rec_bsi")
    wsi_a = arr("L0_rec_Wsi")
    r4 = np.arange(PARTS ** 2)
    pick = np.concatenate([r4[:, None] // PARTS == np.arange(PARTS), r4[:, None] % PARTS == np.arange(PARTS)], 1)
    f32 = np.float32

    def split_rows(w, n):
        return w.reshape(n, P, -1).transpose(1, 0, 2)

    def beside(*parts):
        return np.concatenate([p.reshape(p.shape[0], -1) for p in parts], 1)

    ids = arr("ids").reshape(TILES, 2, PAIRS, P).transpose(3, 0, 2, 1).reshape(P, -1)
    touch = (sample.T[:, :, None] - (P * np.arange(PAIRS) // FIELDS)[None, :, None] == np.arange(TOUCH))
    arrays = {
        "table": np.concatenate(tables, 0),
        "rows_in": beside(np.repeat(starts[field.T], 2, 1), ids, np.zeros_like(ids[:, :2 * PAIRS])),
        "setup": beside(np.eye(P, dtype=f32), (np.eye(P) - 1.0 / P).astype(f32), arr("L0_rec_Ws"),
                        arr("L0_rec_gs")[:, None]),
        "wsi_touch": np.concatenate([wsi_a.T[field].transpose(1, 0, 2), touch.astype(f32)], 2),
        "dense_wd": np.concatenate([split_rows(arr("r_dense_t").T, 2), split_rows(arr("L0_rec_Wd").T, 2),
                                    np.stack([arr("L0_rec_gd"), arr("L0_rec_bd")], 1)[:, :, None]], 2),
        "bias4": np.concatenate([
            np.tile(wsi_a.reshape(1, -1), (PARTS ** 2, 1)),
            np.tile(arr("L0_rec_bs")[None], (PARTS ** 2, 1)), pick.astype(f32)], 1),
        "wl": np.concatenate([wl_pairs, wl_x[:, None]], 1),
        "fold": beside(
            gsi[row_i][:, None], bsi[row_i][:, None],
            np.where(has_x | (part < PROJ), gsi[row_i], f32(1))[:, None], gsi[col], bsi[col],
            (row_i[:, None] == np.arange(PROJ)).astype(f32),
            (col[:, :, None] == np.arange(PROJ)).astype(f32)),
        "second": ((past_block == 0) | (past_block > BLOCKS)).astype(np.int32),
        "biases": beside(arr("b_top1").reshape(-1, P).T, arr("b_top2").reshape(-1, P).T,
                         arr("L0_rec_gl")[:KEPT].reshape(-1, P).T, arr("L0_rec_bl")[:KEPT].reshape(-1, P).T),
        "w1": split_rows(arr("W_top1")[:KEPT], KEPT // P),
        "w1_dense": split_rows(arr("W_top1")[MAXD:], DENSE // P),
        "w2_w3": beside(split_rows(arr("W_top2"), HID1 // P), arr("W_top3").reshape(-1, P).T),
    }
    arrays = {name: np.ascontiguousarray(x) for name, x in arrays.items()}

    nc = bacc.Bacc("TRN2", target_bir_lowering=False, num_devices=1)
    aps = {name: nc.dram_tensor(f"in_{name}", x.shape, mybir.dt.from_np(x.dtype), kind="ExternalInput").ap()
           for name, x in arrays.items()}
    out = nc.dram_tensor("out_y", (1, BATCH), F32, kind="ExternalOutput").ap()
    build(nc, aps, out)
    r = run_bass_kernel_spmd(nc, [{f"in_{name}": x for name, x in arrays.items()}], core_ids=[0])
    return r.results[0]["out_y"].reshape(BATCH, 1)
```
